# Optimizing a Trainium2 kernel written in Bass

```python
import numpy as np
import jax
import jax.numpy as jnp

def _softmax(x, axis=-1):
    return jax.nn.softmax(x, axis=axis)

def _gelu(x):
    return jax.nn.gelu(x, approximate=True)

def _silu(x):
    return jax.nn.silu(x)

def _sigmoid(x):
    return jax.nn.sigmoid(x)

def _layernorm(x, axis=-1, eps=1e-05):
    m = jnp.mean(x, axis=axis, keepdims=True)
    v = jnp.var(x, axis=axis, keepdims=True)
    return (x - m) / jnp.sqrt(v + eps)

def _scatter_add(tgt, idx, src, axis=0):
    return tgt.at[idx].add(src)

def _segment_sum(src, seg, n):
    return jax.ops.segment_sum(src, seg, n)
kernel_name = 'mk_audio_tower_d2_tok_aud1d512_r4_3802d2'

def setup_inputs(seed: int=0):
    np.random.seed(seed)
    _w = jnp.asarray

    def _rec_inputs():
        import jax
        import jax.numpy as jnp
        _rk = jax.random.key(seed)
        x = -0.000928989 + 1.00043 * jax.random.normal(jax.random.fold_in(_rk, 1), (64, 4000), jnp.float32)
        return x
    x = _rec_inputs()

    def _L0_tok_setup():
        import jax, jax.numpy as jnp
        import numpy as np
        SEG_LEN = 48
        STRIDE = SEG_LEN // 2
        CURVATURE = 1.0
        BALL_EPS = 0.004
        MIN_NORM = 1e-15
        key = jax.random.key(seed)
        k1, k2, k3 = jax.random.split(key, 3)
        B, L, D = (128, 2048, 128)
        x_raw = jax.random.normal(k1, (B, L), dtype=jnp.float32)
        W = jax.random.normal(k2, (SEG_LEN, D), dtype=jnp.float32) * (1.0 / np.sqrt(SEG_LEN))
        b = jax.random.normal(k3, (D,), dtype=jnp.float32) * 0.01
        effective_scale = jnp.ones((1,), dtype=jnp.float32)
        return {'x_raw': x_raw, 'W': W, 'b': b, 'effective_scale': effective_scale}
    _L0_tok_all = _L0_tok_setup()
    _L0_tok_in = {k: v for k, v in _L0_tok_all.items() if k in ('W', 'b', 'effective_scale')}
    del _L0_tok_all

    def _L0_attn_setup():
        import jax, jax.numpy as jnp
        import numpy as np
        D_MODEL, N_HEADS, D_KEYS, D_LLM = (128, 8, 16, 1024)
        B, L, S = (32, 256, 250)
        HE = N_HEADS * D_KEYS
        key = jax.random.key(seed)
        ks = jax.random.split(key, 11)
        s = 0.02
        return {'target_embedding': jax.random.normal(ks[0], (B, L, D_MODEL), jnp.float32), 'source_embedding': jax.random.normal(ks[1], (S, D_LLM), jnp.float32), 'value_embedding': jax.random.normal(ks[2], (S, D_LLM), jnp.float32), 'Wq': jax.random.normal(ks[3], (D_MODEL, HE), jnp.float32) * s, 'bq': jnp.zeros((HE,), jnp.float32), 'Wk': jax.random.normal(ks[4], (D_LLM, HE), jnp.float32) * s, 'bk': jnp.zeros((HE,), jnp.float32), 'Wv': jax.random.normal(ks[5], (D_LLM, HE), jnp.float32) * s, 'bv': jnp.zeros((HE,), jnp.float32), 'Wo': jax.random.normal(ks[6], (HE, D_MODEL), jnp.float32) * s, 'bo': jnp.zeros((D_MODEL,), jnp.float32)}
    _L0_attn_all = _L0_attn_setup()
    _L0_attn_in = {k: v for k, v in _L0_attn_all.items() if k in ('source_embedding', 'value_embedding', 'Wq', 'bq', 'Wk', 'bk', 'Wv', 'bv', 'Wo', 'bo')}
    del _L0_attn_all

    def _L0_ffn_setup():
        import jax, jax.numpy as jnp
        import numpy as np
        B, T, D, H = (64, 128, 128, 256)

        def _linear_params(key, out_dim, in_dim):
            kw, kb = jax.random.split(key)
            bound = 1.0 / np.sqrt(in_dim)
            W = jax.random.uniform(kw, (out_dim, in_dim), jnp.float32, -bound, bound)
            b = jax.random.uniform(kb, (out_dim,), jnp.float32, -bound, bound)
            return (W, b)
        key = jax.random.key(seed)
        ks = jax.random.split(key, 8)
        x = jax.random.normal(ks[0], (B, T, D), jnp.float32)
        Wuz, buz = _linear_params(ks[1], H, D)
        Wwz, bwz = _linear_params(ks[2], H, H)
        Wur, bur = _linear_params(ks[3], H, D)
        Wwr, bwr = _linear_params(ks[4], H, H)
        Wu, bu = _linear_params(ks[5], H, D)
        Ww, bw = _linear_params(ks[6], H, H)
        Wo, bo = _linear_params(ks[7], D, H)
        return dict(x=x, Wuz=Wuz, buz=buz, Wwz=Wwz, bwz=bwz, Wur=Wur, bur=bur, Wwr=Wwr, bwr=bwr, Wu=Wu, bu=bu, Ww=Ww, bw=bw, Wo=Wo, bo=bo)
    _L0_ffn_all = _L0_ffn_setup()
    _L0_ffn_in = {k: v for k, v in _L0_ffn_all.items() if k in ('Wuz', 'buz', 'Wwz', 'bwz', 'Wur', 'bur', 'Wwr', 'bwr', 'Wu', 'bu', 'Ww', 'bw', 'Wo', 'bo')}
    del _L0_ffn_all

    def _L1_attn_setup():
        import jax, jax.numpy as jnp
        import numpy as np
        D_MODEL = 128
        NHEAD = 8
        D_FF = 512
        EPS = 1e-05

        def _layernorm(x, gamma, beta):
            mu = jnp.mean(x, axis=-1, keepdims=True)
            var = jnp.mean(jnp.square(x - mu), axis=-1, keepdims=True)
            return (x - mu) * jax.lax.rsqrt(var + EPS) * gamma + beta

        def _rope(x, cos, sin):
            d = x.shape[-1]
            x1, x2 = (x[..., :d // 2], x[..., d // 2:])
            return jnp.concatenate([x1 * cos - x2 * sin, x2 * cos + x1 * sin], axis=-1)
        key = jax.random.key(seed)
        ks = jax.random.split(key, 12)
        B, S = (2, 1024)
        s = 0.02
        inp = {'src': jax.random.normal(ks[0], (B, S, D_MODEL), dtype=jnp.float32), 'Wq': jax.random.normal(ks[1], (D_MODEL, D_MODEL), dtype=jnp.float32) * s, 'Wk': jax.random.normal(ks[2], (D_MODEL, D_MODEL), dtype=jnp.float32) * s, 'Wv': jax.random.normal(ks[3], (D_MODEL, D_MODEL), dtype=jnp.float32) * s, 'Wo': jax.random.normal(ks[4], (D_MODEL, D_MODEL), dtype=jnp.float32) * s, 'W1': jax.random.normal(ks[5], (D_FF, D_MODEL), dtype=jnp.float32) * s, 'b1': jnp.zeros((D_FF,), dtype=jnp.float32), 'W2': jax.random.normal(ks[6], (D_MODEL, D_FF), dtype=jnp.float32) * s, 'b2': jnp.zeros((D_MODEL,), dtype=jnp.float32), 'g1': jnp.ones((D_MODEL,), dtype=jnp.float32), 'be1': jnp.zeros((D_MODEL,), dtype=jnp.float32), 'g2': jnp.ones((D_MODEL,), dtype=jnp.float32), 'be2': jnp.zeros((D_MODEL,), dtype=jnp.float32)}
        return inp
    _L1_attn_all = _L1_attn_setup()
    _L1_attn_in = {k: v for k, v in _L1_attn_all.items() if k in ('Wq', 'Wk', 'Wv', 'Wo', 'W1', 'b1', 'W2', 'b2', 'g1', 'be1', 'g2', 'be2')}
    del _L1_attn_all

    def _L1_ffn_setup():
        import jax, jax.numpy as jnp
        import numpy as np
        B, S, D = (4, 512, 128)
        I = 96
        E = 16
        K = 2

        def _inv_softplus(v):
            return float(np.log(np.expm1(v)))

        def swiglu5(h, alpha, gate_scale, up_shift, gate_clamp_raw, up_clamp_raw):
            gate_clamp = jax.nn.softplus(gate_clamp_raw)
            up_clamp = jax.nn.softplus(up_clamp_raw)
            g = jnp.clip(h[..., ::2], -gate_clamp, gate_clamp)
            u = jnp.clip(h[..., 1::2], -up_clamp, up_clamp)
            return g * jax.nn.sigmoid(g * alpha) * gate_scale * (u + up_shift)
        key = jax.random.key(seed)
        ks = jax.random.split(key, 10)
        std = 0.02
        raw = _inv_softplus(7.0)
        act = jnp.array([1.702, 1.0, 1.0, raw, raw], dtype=jnp.float32)
        return {'x': jax.random.normal(ks[0], (B, S, D), dtype=jnp.float32), 'gate_w': jax.random.normal(ks[1], (D, E), dtype=jnp.float32) * 0.01, 'gate_b': jnp.zeros((E,), dtype=jnp.float32), 'shared_w1': jax.random.normal(ks[2], (D, 2 * I), dtype=jnp.float32) * std, 'shared_b1': jnp.zeros((2 * I,), dtype=jnp.float32), 'shared_w2': jax.random.normal(ks[3], (I, D), dtype=jnp.float32) * std, 'shared_b2': jnp.zeros((D,), dtype=jnp.float32), 'shared_act': act, 'expert_w1': jax.random.normal(ks[4], (E, D, 2 * I), dtype=jnp.float32) * std, 'expert_b1': jnp.zeros((E, 2 * I), dtype=jnp.float32), 'expert_w2': jax.random.normal(ks[5], (E, I, D), dtype=jnp.float32) * std, 'expert_b2': jnp.zeros((E, D), dtype=jnp.float32), 'expert_act': jnp.tile(act[None, :], (E, 1))}
    _L1_ffn_all = _L1_ffn_setup()
    _L1_ffn_in = {k: v for k, v in _L1_ffn_all.items() if k in ('gate_w', 'gate_b', 'shared_w1', 'shared_b1', 'shared_w2', 'shared_b2', 'shared_act', 'expert_w1', 'expert_b1', 'expert_w2', 'expert_b2', 'expert_act')}
    del _L1_ffn_all
    return {'x': x, 'L0_tok_W': _L0_tok_in['W'], 'L0_tok_b': _L0_tok_in['b'], 'L0_tok_effective_scale': _L0_tok_in['effective_scale'], 'L0_attn_source_embedding': _L0_attn_in['source_embedding'], 'L0_attn_value_embedding': _L0_attn_in['value_embedding'], 'L0_attn_Wq': _L0_attn_in['Wq'], 'L0_attn_bq': _L0_attn_in['bq'], 'L0_attn_Wk': _L0_attn_in['Wk'], 'L0_attn_bk': _L0_attn_in['bk'], 'L0_attn_Wv': _L0_attn_in['Wv'], 'L0_attn_bv': _L0_attn_in['bv'], 'L0_attn_Wo': _L0_attn_in['Wo'], 'L0_attn_bo': _L0_attn_in['bo'], 'L0_ffn_Wuz': _L0_ffn_in['Wuz'], 'L0_ffn_buz': _L0_ffn_in['buz'], 'L0_ffn_Wwz': _L0_ffn_in['Wwz'], 'L0_ffn_bwz': _L0_ffn_in['bwz'], 'L0_ffn_Wur': _L0_ffn_in['Wur'], 'L0_ffn_bur': _L0_ffn_in['bur'], 'L0_ffn_Wwr': _L0_ffn_in['Wwr'], 'L0_ffn_bwr': _L0_ffn_in['bwr'], 'L0_ffn_Wu': _L0_ffn_in['Wu'], 'L0_ffn_bu': _L0_ffn_in['bu'], 'L0_ffn_Ww': _L0_ffn_in['Ww'], 'L0_ffn_bw': _L0_ffn_in['bw'], 'L0_ffn_Wo': _L0_ffn_in['Wo'], 'L0_ffn_bo': _L0_ffn_in['bo'], 'L1_attn_Wq': _L1_attn_in['Wq'], 'L1_attn_Wk': _L1_attn_in['Wk'], 'L1_attn_Wv': _L1_attn_in['Wv'], 'L1_attn_Wo': _L1_attn_in['Wo'], 'L1_attn_W1': _L1_attn_in['W1'], 'L1_attn_b1': _L1_attn_in['b1'], 'L1_attn_W2': _L1_attn_in['W2'], 'L1_attn_b2': _L1_attn_in['b2'], 'L1_attn_g1': _L1_attn_in['g1'], 'L1_attn_be1': _L1_attn_in['be1'], 'L1_attn_g2': _L1_attn_in['g2'], 'L1_attn_be2': _L1_attn_in['be2'], 'L1_ffn_gate_w': _L1_ffn_in['gate_w'], 'L1_ffn_gate_b': _L1_ffn_in['gate_b'], 'L1_ffn_shared_w1': _L1_ffn_in['shared_w1'], 'L1_ffn_shared_b1': _L1_ffn_in['shared_b1'], 'L1_ffn_shared_w2': _L1_ffn_in['shared_w2'], 'L1_ffn_shared_b2': _L1_ffn_in['shared_b2'], 'L1_ffn_shared_act': _L1_ffn_in['shared_act'], 'L1_ffn_expert_w1': _L1_ffn_in['expert_w1'], 'L1_ffn_expert_b1': _L1_ffn_in['expert_b1'], 'L1_ffn_expert_w2': _L1_ffn_in['expert_w2'], 'L1_ffn_expert_b2': _L1_ffn_in['expert_b2'], 'L1_ffn_expert_act': _L1_ffn_in['expert_act']}

def reference(x, L0_tok_W, L0_tok_b, L0_tok_effective_scale, L0_attn_source_embedding, L0_attn_value_embedding, L0_attn_Wq, L0_attn_bq, L0_attn_Wk, L0_attn_bk, L0_attn_Wv, L0_attn_bv, L0_attn_Wo, L0_attn_bo, L0_ffn_Wuz, L0_ffn_buz, L0_ffn_Wwz, L0_ffn_bwz, L0_ffn_Wur, L0_ffn_bur, L0_ffn_Wwr, L0_ffn_bwr, L0_ffn_Wu, L0_ffn_bu, L0_ffn_Ww, L0_ffn_bw, L0_ffn_Wo, L0_ffn_bo, L1_attn_Wq, L1_attn_Wk, L1_attn_Wv, L1_attn_Wo, L1_attn_W1, L1_attn_b1, L1_attn_W2, L1_attn_b2, L1_attn_g1, L1_attn_be1, L1_attn_g2, L1_attn_be2, L1_ffn_gate_w, L1_ffn_gate_b, L1_ffn_shared_w1, L1_ffn_shared_b1, L1_ffn_shared_w2, L1_ffn_shared_b2, L1_ffn_shared_act, L1_ffn_expert_w1, L1_ffn_expert_b1, L1_ffn_expert_w2, L1_ffn_expert_b2, L1_ffn_expert_act):
    import jax
    import jax.numpy as jnp

    def _L0_tok_ref(x_raw, W, b, effective_scale):
        import jax, jax.numpy as jnp
        import numpy as np
        SEG_LEN = 48
        STRIDE = SEG_LEN // 2
        CURVATURE = 1.0
        BALL_EPS = 0.004
        MIN_NORM = 1e-15
        B, L = x_raw.shape
        seg_len, D = W.shape
        N = (L - seg_len) // STRIDE + 1
        idx = jnp.arange(N)[:, None] * STRIDE + jnp.arange(seg_len)[None, :]
        segs = x_raw[:, idx]
        z = jnp.einsum('bnl,ld->bnd', segs, W) + b
        scale = jnp.tanh(effective_scale[0])
        u = z * scale
        sqrt_c = jnp.sqrt(jnp.float32(CURVATURE))
        u_norm = jnp.maximum(jnp.linalg.norm(u, axis=-1, keepdims=True), MIN_NORM)
        y = jnp.tanh(sqrt_c * u_norm) * u / (sqrt_c * u_norm)
        y_norm = jnp.maximum(jnp.linalg.norm(y, axis=-1, keepdims=True), MIN_NORM)
        maxnorm = (1.0 - BALL_EPS) / sqrt_c
        y = jnp.where(y_norm > maxnorm, y / y_norm * maxnorm, y)
        return y

    def _L0_attn_ref(target_embedding, source_embedding, value_embedding, Wq, bq, Wk, bk, Wv, bv, Wo, bo):
        import jax, jax.numpy as jnp
        import numpy as np
        D_MODEL, N_HEADS, D_KEYS, D_LLM = (128, 8, 16, 1024)
        B, L, S = (32, 256, 250)
        HE = N_HEADS * D_KEYS
        H, E = (N_HEADS, D_KEYS)
        Bb, Ll, _ = target_embedding.shape
        Ss = source_embedding.shape[0]
        q = (target_embedding @ Wq + bq).reshape(Bb, Ll, H, E)
        k = (source_embedding @ Wk + bk).reshape(Ss, H, E)
        v = (value_embedding @ Wv + bv).reshape(Ss, H, E)
        scale = 1.0 / jnp.sqrt(jnp.asarray(E, q.dtype))
        scores = jnp.einsum('blhe,she->bhls', q, k)
        attn = jax.nn.softmax(scale * scores, axis=-1)
        out = jnp.einsum('bhls,she->blhe', attn, v).reshape(Bb, Ll, H * E)
        return out @ Wo + bo

    def _L0_ffn_ref(x, Wuz, buz, Wwz, bwz, Wur, bur, Wwr, bwr, Wu, bu, Ww, bw, Wo, bo):
        import jax, jax.numpy as jnp
        import numpy as np
        B, T, D, H = (64, 128, 128, 256)

        def _linear_params(key, out_dim, in_dim):
            kw, kb = jax.random.split(key)
            bound = 1.0 / np.sqrt(in_dim)
            W = jax.random.uniform(kw, (out_dim, in_dim), jnp.float32, -bound, bound)
            b = jax.random.uniform(kb, (out_dim,), jnp.float32, -bound, bound)
            return (W, b)
        b_, t_, _ = x.shape
        h_dim = Wwz.shape[0]
        xz = (jnp.einsum('btd,hd->bth', x, Wuz) + buz).transpose(1, 0, 2)
        xr = (jnp.einsum('btd,hd->bth', x, Wur) + bur).transpose(1, 0, 2)
        xc = (jnp.einsum('btd,hd->bth', x, Wu) + bu).transpose(1, 0, 2)

        def step(h, inp):
            xz_t, xr_t, xc_t = inp
            z = jax.nn.sigmoid(xz_t + h @ Wwz.T + bwz)
            r = jax.nn.sigmoid(xr_t + h @ Wwr.T + bwr)
            c = jnp.tanh(xc_t + h * r @ Ww.T + bw)
            h_new = z * h + (1.0 - z) * c
            return (h_new, h_new)
        h0 = jnp.zeros((b_, h_dim), x.dtype)
        _, hs = jax.lax.scan(step, h0, (xz, xr, xc))
        out = jax.nn.sigmoid(jnp.einsum('tbh,dh->btd', hs, Wo) + bo)
        return out

    def _L1_attn_ref(src, Wq, Wk, Wv, Wo, W1, b1, W2, b2, g1, be1, g2, be2):
        import jax, jax.numpy as jnp
        import numpy as np
        D_MODEL = 128
        NHEAD = 8
        D_FF = 512
        EPS = 1e-05

        def _layernorm(x, gamma, beta):
            mu = jnp.mean(x, axis=-1, keepdims=True)
            var = jnp.mean(jnp.square(x - mu), axis=-1, keepdims=True)
            return (x - mu) * jax.lax.rsqrt(var + EPS) * gamma + beta

        def _rope(x, cos, sin):
            d = x.shape[-1]
            x1, x2 = (x[..., :d // 2], x[..., d // 2:])
            return jnp.concatenate([x1 * cos - x2 * sin, x2 * cos + x1 * sin], axis=-1)
        B, S, D = src.shape
        H = NHEAD
        hd = D // H
        q = (src @ Wq.T).reshape(B, S, H, hd)
        k = (src @ Wk.T).reshape(B, S, H, hd)
        v = (src @ Wv.T).reshape(B, S, H, hd)
        inv_freq = 1.0 / 10000.0 ** (jnp.arange(0, hd, 2, dtype=jnp.float32) / hd)
        t = jnp.arange(S, dtype=jnp.float32)
        freqs = t[:, None] * inv_freq[None, :]
        cos = jnp.cos(freqs)[None, :, None, :]
        sin = jnp.sin(freqs)[None, :, None, :]
        q = _rope(q, cos, sin)
        k = _rope(k, cos, sin)
        scale = 1.0 / jnp.sqrt(jnp.float32(hd))
        scores = jnp.einsum('bqhd,bkhd->bhqk', q, k) * scale
        attn = jax.nn.softmax(scores, axis=-1)
        ctx = jnp.einsum('bhqk,bkhd->bqhd', attn, v).reshape(B, S, D)
        attn_out = ctx @ Wo.T
        x = _layernorm(src + attn_out, g1, be1)
        ffn = jax.nn.relu(x @ W1.T + b1) @ W2.T + b2
        x = _layernorm(x + ffn, g2, be2)
        return x

    def _L1_ffn_ref(x, gate_w, gate_b, shared_w1, shared_b1, shared_w2, shared_b2, shared_act, expert_w1, expert_b1, expert_w2, expert_b2, expert_act):
        import jax, jax.numpy as jnp
        import numpy as np
        B, S, D = (4, 512, 128)
        I = 96
        E = 16
        K = 2

        def _inv_softplus(v):
            return float(np.log(np.expm1(v)))

        def swiglu5(h, alpha, gate_scale, up_shift, gate_clamp_raw, up_clamp_raw):
            gate_clamp = jax.nn.softplus(gate_clamp_raw)
            up_clamp = jax.nn.softplus(up_clamp_raw)
            g = jnp.clip(h[..., ::2], -gate_clamp, gate_clamp)
            u = jnp.clip(h[..., 1::2], -up_clamp, up_clamp)
            return g * jax.nn.sigmoid(g * alpha) * gate_scale * (u + up_shift)
        shape = x.shape
        xf = x.reshape(-1, shape[-1])
        h = xf @ shared_w1 + shared_b1
        t = swiglu5(h, shared_act[0], shared_act[1], shared_act[2], shared_act[3], shared_act[4])
        z = t @ shared_w2 + shared_b2
        gate_logits = xf @ gate_w + gate_b
        gate_probs = jax.nn.softmax(gate_logits, -1)
        w, idx = jax.lax.top_k(gate_probs, K)
        w = w / jnp.sum(w, axis=-1, keepdims=True)
        cw = jnp.sum(jax.nn.one_hot(idx, E, dtype=xf.dtype) * w[..., None], axis=1)
        he = jnp.einsum('nd,edh->enh', xf, expert_w1) + expert_b1[:, None, :]
        a = expert_act
        te = swiglu5(he, a[:, 0, None, None], a[:, 1, None, None], a[:, 2, None, None], a[:, 3, None, None], a[:, 4, None, None])
        oe = jnp.einsum('enh,ehd->end', te, expert_w2) + expert_b2[:, None, :]
        y = jnp.einsum('ne,end->nd', cw, oe)
        return (y + z).reshape(shape)
    h = _L0_tok_ref(x, L0_tok_W, L0_tok_b, L0_tok_effective_scale)
    h = h + _L0_attn_ref(_layernorm(h, axis=-1), L0_attn_source_embedding, L0_attn_value_embedding, L0_attn_Wq, L0_attn_bq, L0_attn_Wk, L0_attn_bk, L0_attn_Wv, L0_attn_bv, L0_attn_Wo, L0_attn_bo)
    h = h + _L0_ffn_ref(_layernorm(h, axis=-1), L0_ffn_Wuz, L0_ffn_buz, L0_ffn_Wwz, L0_ffn_bwz, L0_ffn_Wur, L0_ffn_bur, L0_ffn_Wwr, L0_ffn_bwr, L0_ffn_Wu, L0_ffn_bu, L0_ffn_Ww, L0_ffn_bw, L0_ffn_Wo, L0_ffn_bo)
    h = h + _L1_attn_ref(_layernorm(h, axis=-1), L1_attn_Wq, L1_attn_Wk, L1_attn_Wv, L1_attn_Wo, L1_attn_W1, L1_attn_b1, L1_attn_W2, L1_attn_b2, L1_attn_g1, L1_attn_be1, L1_attn_g2, L1_attn_be2)
    h = h + _L1_ffn_ref(_layernorm(h, axis=-1), L1_ffn_gate_w, L1_ffn_gate_b, L1_ffn_shared_w1, L1_ffn_shared_b1, L1_ffn_shared_w2, L1_ffn_shared_b2, L1_ffn_shared_act, L1_ffn_expert_w1, L1_ffn_expert_b1, L1_ffn_expert_w2, L1_ffn_expert_b2, L1_ffn_expert_act)
    return h

_drawn_inputs = setup_inputs


def setup_inputs(seed=0):
    import zlib

    import numpy as np

    out = dict(_drawn_inputs(seed))
    spreads = {'L0_attn_bq': (0.0, 0.8),
     'L0_attn_bk': (0.0, 0.8),
     'L0_attn_bv': (0.0, 0.1),
     'L0_attn_bo': (0.0, 0.1),
     'L1_attn_b1': (0.0, 0.35),
     'L1_attn_b2': (0.0, 0.1),
     'L1_attn_g1': (1.0, 0.2),
     'L1_attn_be1': (0.0, 0.1),
     'L1_attn_g2': (1.0, 0.2),
     'L1_attn_be2': (0.0, 0.1),
     'L1_ffn_gate_b': (0.0, 0.1),
     'L1_ffn_shared_b1': (0.0, 0.8),
     'L1_ffn_shared_b2': (0.0, 0.1),
     'L1_ffn_expert_b1': (0.0, 0.8),
     'L1_ffn_expert_b2': (0.0, 0.1)}
    factors = {'L0_tok_b': 7.022,
     'L0_attn_source_embedding': 5.459,
     'L0_attn_Wq': 5.712,
     'L0_attn_Wk': 5.055,
     'L0_ffn_buz': 8.0,
     'L0_ffn_Wwz': 3.128,
     'L0_ffn_bwz': 8.0,
     'L0_ffn_Wur': 3.3,
     'L0_ffn_bur': 8.0,
     'L0_ffn_Wwr': 6.546,
     'L0_ffn_bwr': 8.0,
     'L1_attn_Wq': 8.0,
     'L1_attn_Wk': 8.0,
     'L1_ffn_shared_w1': 3.147,
     'L1_ffn_shared_w2': 3.072,
     'L1_ffn_expert_w1': 4.278,
     'L1_ffn_expert_w2': 4.097}
    for name, (base, spread) in spreads.items():
        noise = np.random.default_rng([zlib.crc32(name.encode()), seed]).standard_normal(out[name].shape)
        drawn = base * np.exp(spread * noise) if base else spread * noise
        out[name] = jnp.asarray(drawn.astype(out[name].dtype))
    for name, factor in factors.items():
        out[name] = (out[name] * factor).astype(out[name].dtype)
    return out
```

```python
from contextlib import ExitStack

import numpy as np
import concourse.bass as bass
from concourse import mybir

F32 = mybir.dt.float32
BF16 = mybir.dt.bfloat16
F16 = mybir.dt.float16
ALU = mybir.AluOpType
ACT = mybir.ActivationFunctionType
AX = mybir.AxisListType

P = 128
D = 128
BATCH = 64
SEG, STRIDE = 48, 24
STEPS = (4000 - SEG) // STRIDE + 1
TOKENS = BATCH * STEPS
TILE = 480
TILES = TOKENS // TILE
HEADS, HD = 8, 16
SLOT = 32
GROUPS = HEADS * SLOT // P
GH = HEADS // GROUPS
LLM, SRC = 1024, 250
KC = LLM // P
HID = 256
DFF = 512
EXPERTS, INTER = 16, 96
BLOCK_STEPS = 5
BALL = 1.0 - 0.004
LN_EPS = 1e-5
BANK = 512


class Signals:

    def __init__(self, nc, ctx):
        self.nc, self.ctx, self.all = nc, ctx, []

    def __call__(self, name):
        self.all.append(self.ctx.enter_context(self.nc.semaphore(name)))
        return self.all[-1]

    def clear(self):
        with self.nc.Block() as block:
            @block.gpsimd
            def _(pool):
                for s in self.all:
                    pool.sem_clear(s)


class Norm:

    def __init__(self, nc, sem, name, mean_ps, var_ps, centered, squares, rstd, ones, eps):
        self.nc, self.eps = nc, eps
        self.mean_ps, self.var_ps = mean_ps, var_ps
        self.centered, self.squares, self.rstd, self.ones = centered, squares, rstd, ones
        self.mean_ready = sem(name + "_mean_ready")
        self.centered_ready = sem(name + "_centered_ready")
        self.squares_ready = sem(name + "_squares_ready")
        self.var_ready = sem(name + "_var_ready")
        self.log_ready = sem(name + "_log_ready")
        self.rstd_ready = sem(name + "_rstd_ready")
        self.done = sem(name + "_done")

    def pe_mean(self, src):
        self.nc.tensor.matmul(self.mean_ps, self.ones, src, start=True, stop=True).then_inc(self.mean_ready, 1)

    def pe_var(self, pe, n):
        pe.wait_ge(self.squares_ready, n)
        self.nc.tensor.matmul(self.var_ps, self.ones, self.squares, start=True, stop=True).then_inc(self.var_ready, 1)

    def act(self, act, n):
        self.act_square(act, n)
        self.act_rstd(act, n)

    def act_square(self, act, n):
        act.wait_ge(self.centered_ready, n)
        self.nc.scalar.activation(self.squares, self.centered, ACT.Square).then_inc(self.squares_ready, 1)

    def act_rstd(self, act, n):
        act.wait_ge(self.var_ready, n)
        self.nc.scalar.activation(self.rstd, self.var_ps, ACT.Ln, bias=self.eps).then_inc(self.log_ready, 1)
        act.wait_ge(self.log_ready, n)
        self.nc.scalar.activation(self.rstd, self.rstd, ACT.Exp, scale=-0.5).then_inc(self.rstd_ready, 1)

    def dve(self, dve, n, src, dst):
        self.dve_center(dve, n, src)
        self.dve_scale(dve, n, dst)

    def dve_center(self, dve, n, src):
        dve.wait_ge(self.mean_ready, n)
        self.nc.vector.tensor_tensor(self.centered, src, self.mean_ps, ALU.subtract).then_inc(self.centered_ready, 1)

    def dve_scale(self, dve, n, dst):
        dve.wait_ge(self.rstd_ready, n)
        self.nc.vector.tensor_tensor(dst, self.centered, self.rstd, ALU.mult).then_inc(self.done, 1)


class Attention:

    def __init__(self, nc, sem, name, ps, width, queries, keys, keys_wide, exp_units, bufs, eps):
        self.nc, self.ps, self.width, self.eps = nc, ps, width, eps
        self.queries, self.keys, self.keys_wide, self.exp_units = queries, keys, keys_wide, exp_units
        self.qs, self.ks, self.maxima, self.max_parts, self.max_rows, self.probs, self.outs, self.rden, self.normed, self.sel, self.ident = bufs
        self.stack_loaded = sem(name + "_stack_loaded")
        self.scores_ready = sem(name + "_scores_ready")
        self.max_ready = sem(name + "_max_ready")
        self.max_part_ready = sem(name + "_max_part_ready")
        self.max_parts_ready = sem(name + "_max_parts_ready")
        self.max_turned = sem(name + "_max_turned")
        self.max_rows_ready = sem(name + "_max_rows_ready")
        self.max_rows_kept = sem(name + "_max_rows_kept")
        self.max_rows_loaded = sem(name + "_max_rows_loaded")
        self.logits_ready = sem(name + "_logits_ready")
        self.probs_ready = sem(name + "_probs_ready")
        self.values_done = sem(name + "_values_done")
        self.outs_ready = sem(name + "_outs_ready")
        self.denom_ready = sem(name + "_denom_ready")
        self.log_ready = sem(name + "_log_ready")
        self.rden_ready = sem(name + "_rden_ready")
        self.normed_ready = sem(name + "_normed_ready")
        self.NM, self.NU = 2 * len(queries), len(exp_units)

    def pe_scores(self, pe, i, k, u):
        q0, qn, k0 = self.queries[u // 2]
        if u == 0:
            self.wait_stack(pe, i)
        else:
            pe.wait_ge(self.max_ready, i * self.NM + u)
        for n in range(4):
            h = 4 * (u % 2) + n
            last = self.nc.tensor.matmul(
                self.ps[0:qn, n // 2, (n % 2) * self.keys_wide:(n % 2 + 1) * self.keys_wide],
                self.qs[0:6 * HD, k, h, q0:q0 + qn], self.ks[0:6 * HD, k * (self.ks.shape[1] - 1), h, k0:k0 + self.keys_wide],
                start=True, stop=True)
        last.then_inc(self.scores_ready, 1)

    def dve_max(self, dve, i, u):
        q0, qn, _ = self.queries[u // 2]
        W = self.keys_wide
        dve.wait_ge(self.scores_ready, i * self.NM + u + 1)
        src = self.ps[0:qn, 0:2, 0:2 * W].rearrange("p b (s k) -> p b s k", k=W)
        dst = self.maxima[0:qn, u // 2, 4 * (u % 2):4 * (u % 2) + 4].rearrange("p (b s) -> p b s", s=2)
        self.nc.vector.tensor_reduce(dst, src, AX.X, ALU.max).then_inc(self.max_ready, 1)

    def dve_max_parts(self, dve, i):
        v, m, parts = self.nc.vector, self.maxima[:], self.max_parts
        dve.wait_ge(self.max_ready, (i + 1) * self.NM)
        for part in range(3):
            v.tensor_copy(parts[:, :, part, :], m).then_inc(self.max_part_ready, 1)
            dve.wait_ge(self.max_part_ready, 5 * i + 2 * part + 1)
            if part < 2:
                v.tensor_tensor(m, m, parts[:, :, part, :], ALU.subtract).then_inc(self.max_part_ready, 1)
                dve.wait_ge(self.max_part_ready, 5 * i + 2 * part + 2)

    def pe_turn(self, pe, i):
        pe.wait_ge(self.max_part_ready, 5 * i + 5)
        for b, (q0, qn, _) in enumerate(self.queries):
            last = self.nc.tensor.transpose(self.turned[:, b, 0:qn],
                                            self.max_parts[0:qn, b, :, :].rearrange("p a h -> p (a h)"), self.ident[0:qn, 0:qn])
        last.then_inc(self.max_turned, 1)

    def dve_rows(self, dve, i):
        dve.wait_ge(self.max_turned, i + 1)
        for dst, src in self.row_copies:
            self.nc.vector.tensor_copy(dst, src).then_inc(self.max_rows_ready, 1)

    def sp_rows(self, sp, i, k, kept):
        sp.wait_ge(self.max_rows_ready, len(self.row_copies) * (i + 1))
        sp.dma_start(kept, self.max_rows[:]).then_inc(self.max_rows_kept, 16)
        sp.wait_ge(self.max_rows_kept, 16 * (i + 1))
        sp.dma_start(self.qs[6 * HD:6 * HD + 3, k, :, :], kept.rearrange("(a h) n -> a h n", h=HEADS)).then_inc(self.max_rows_loaded, 16)

    def pe_logits(self, pe, i, k, u):
        heads, q0, qn, chunks = self.exp_units[u]
        if u == 0:
            pe.wait_ge(self.max_rows_loaded, 16 * (i + 1))
        if u >= 2:
            pe.wait_ge(self.probs_ready, i * self.NU + u - 1)
        for n, (k0, kn, _, _, _) in enumerate(chunks):
            for b, h in enumerate(heads):
                last = self.nc.tensor.matmul(self.ps[0:kn, 2 + 2 * (u % 2) + b, n * qn:(n + 1) * qn],
                                             self.ks[0:6 * HD + 3, k * (self.ks.shape[1] - 1), h, k0:k0 + kn],
                                             self.qs[0:6 * HD + 3, k, h, q0:q0 + qn], start=True, stop=True)
        last.then_inc(self.logits_ready, 1)

    def pe_values(self, pe, i, k, u, values):
        heads, q0, qn, chunks = self.exp_units[u]
        pe.wait_ge(self.probs_ready, i * self.NU + u + 1)
        for n, (_, kn, v, first, stop) in enumerate(chunks):
            for b, h in enumerate(heads):
                j, g = h % GH, h // GH
                last = self.nc.tensor.matmul(self.ps[SLOT * j:SLOT * j + SLOT, 6 + g, q0:q0 + qn],
                                             values(k, v)[0:kn, h * SLOT:(h + 1) * SLOT],
                                             self.probs[0:kn, u % 3, b, n * qn:(n + 1) * qn], start=first, stop=stop)
        last.then_inc(self.values_done, 1)

    def pe_denominators(self, pe, i):
        for g in range(GROUPS):
            pe.wait_ge(self.outs_ready, GROUPS * (i + 1))
            self.nc.tensor.matmul(self.ps[:, 6 + g, 0:self.width], self.sel, self.outs[:, g, :], start=True, stop=True).then_inc(self.denom_ready, 1)

    def act_probs(self, act, i, u):
        heads, q0, qn, chunks = self.exp_units[u]
        kn, w = chunks[0][1], len(chunks) * qn
        act.wait_ge(self.logits_ready, i * self.NU + u + 1)
        if u >= 3:
            act.wait_ge(self.values_done, i * self.NU + u - 2)
        self.nc.scalar.activation(self.probs[0:kn, u % 3, :, 0:w], self.ps[0:kn, 2 + 2 * (u % 2):4 + 2 * (u % 2), 0:w], ACT.Exp,
                                  scale=HD ** -0.5).then_inc(self.probs_ready, 1)

    def act_outs(self, act, i):
        nc = self.nc
        act.wait_ge(self.values_done, (i + 1) * self.NU)
        for g in range(GROUPS):
            nc.scalar.activation(self.outs[:, g, :], self.ps[:, 6 + g, 0:self.width], ACT.Copy).then_inc(self.outs_ready, 1)
        for g in range(GROUPS):
            act.wait_ge(self.denom_ready, GROUPS * i + g + 1)
            nc.scalar.activation(self.rden[:, g, :], self.ps[:, 6 + g, 0:self.width], ACT.Ln).then_inc(self.log_ready, 1)
            act.wait_ge(self.log_ready, GROUPS * i + g + 1)
            nc.scalar.activation(self.rden[:, g, :], self.rden[:, g, :], ACT.Exp, scale=-1.0).then_inc(self.rden_ready, 1)

    def dve_normed(self, dve, i):
        for g in range(GROUPS):
            dve.wait_ge(self.rden_ready, GROUPS * i + g + 1)
            self.nc.vector.tensor_tensor(self.normed[:, g, :], self.outs[:, g, :], self.rden[:, g, :], ALU.mult).then_inc(self.normed_ready, 1)


class Split:

    def __init__(self, nc, sem, name, full, rest, parts, kept, order, zeros):
        self.zeros = zeros
        self.nc, self.full, self.rest, self.parts, self.kept, self.order = nc, full, rest, parts, kept, order
        self.full_ready = sem(name + "_full_ready")
        self.part_ready = sem(name + "_part_ready")
        self.rest_ready = sem(name + "_rest_ready")
        self.stored = sem(name + "_stored")

    def pool(self, pool, n):
        g = self.nc.gpsimd
        pool.wait_ge(self.full_ready, n + 1)
        g.tensor_tensor(self.parts[:, 0, :], self.full, self.zeros, ALU.add).then_inc(self.part_ready, 1)
        pool.wait_ge(self.part_ready, 3 * n + 1)
        g.tensor_tensor(self.parts[:, 1, :], self.full, self.parts[:, 0, :], ALU.subtract).then_inc(self.part_ready, 1)
        pool.wait_ge(self.part_ready, 3 * n + 2)
        g.tensor_tensor(self.rest, self.full, self.parts[:, 0, :], ALU.subtract).then_inc(self.rest_ready, 1)
        pool.wait_ge(self.rest_ready, n + 1)
        g.tensor_tensor(self.parts[:, 2, :], self.rest, self.parts[:, 1, :], ALU.subtract).then_inc(self.part_ready, 1)

    def sp(self, sp, n, stack, loaded):
        sp.wait_ge(self.part_ready, 3 * n + 3)
        sp.dma_start(self.kept, self.parts[:]).then_inc(self.stored, 16)
        sp.wait_ge(self.stored, 16 * (n + 1))
        for r, part in enumerate(self.order):
            sp.dma_start(stack[HD * r:HD * (r + 1)], self.kept[:, part, :].rearrange("(h e) n -> e h n", e=HD)).then_inc(loaded, 16)


Q_ORDER = (0, 0, 0, 1, 1, 2)
K_ORDER = (0, 1, 2, 0, 1, 0)


SIGMOID_SET = 2
LN_EXP_SET = 6


def load_tables(nc, act, table_set):
    act.add_instruction(mybir.InstLoadActFuncSet(act_func_set_id=table_set, name=nc.get_next_instruction_name(), engine=mybir.EngineType.Activation))


def load(eng, sem, pairs):
    for dst, src in pairs:
        eng.dma_start(dst, src).then_inc(sem, 16)
    return 16 * len(pairs)


def stage_tokenizer(nc, io, hA, segs, ps, C):
    with ExitStack() as ctx:
        sb = lambda name, shape: ctx.enter_context(nc.sbuf_tensor(name, shape, F32))
        sem = Signals(nc, ctx)
        w, b, sc = sb("tok_w", [SEG, D]), sb("tok_b", [P, 1]), sb("tok_scale", [P, 1])
        u, sq = sb("tok_u", [P, 2, TILE]), sb("tok_sq", [P, 2, TILE])
        lg, nrm, rn, f = sb("tok_log", [P, 2, TILE]), sb("tok_norm", [P, 2, TILE]), sb("tok_rnorm", [P, 2, TILE]), sb("tok_factor", [P, 2, TILE])
        loaded, scale_ready = sem("tok_loaded"), sem("tok_scale_ready")
        z_ready, u_ready, sq_ready, ss_ready = sem("tok_z_ready"), sem("tok_u_ready"), sem("tok_sq_ready"), sem("tok_ss_ready")
        clamped, log_ready, norm_ready, tanh_ready = sem("tok_clamped"), sem("tok_log_ready"), sem("tok_norm_ready"), sem("tok_tanh_ready")
        factor_ready, h_ready = sem("tok_factor_ready"), sem("tok_h_ready")
        half = STEPS * BATCH
        total = 16 * (5 + len(C["loads"]))
        with nc.Block() as block:
            @block.sync
            def _(sp):
                load(sp, loaded, [(w[:], io["tok_W"]), (b[:], io["tok_b"]), (sc[:], io["tok_scale"].broadcast_to([P, 1])),
                                  (segs[0:STRIDE, :], io["x"][:, 0:STEPS, :].rearrange("l n b -> l (n b)")),
                                  (segs[STRIDE:SEG, :], io["x"][:, 1:STEPS + 1, :].rearrange("l n b -> l (n b)"))])
                load(sp, loaded, C["loads"])
                sp.wait_ge(loaded, total)

            @block.tensor
            def _(pe):
                pe.wait_ge(loaded, total)
                with pe.Fori(0, TILES // 2) as i:
                    pe.wait_ge(h_ready, 2 * i + 1)
                    for k in range(2):
                        nc.tensor.matmul(ps[:, k, 0:TILE], w[:], segs[0:SEG, bass.ds(i * 2 * TILE + k * TILE, TILE)], start=True, stop=True).then_inc(z_ready, 1)
                    for k in range(2):
                        pe.wait_ge(sq_ready, 2 * i + k + 1)
                        nc.tensor.matmul(ps[:, 2 + k, 0:TILE], C["ones"], sq[:, k, :], start=True, stop=True).then_inc(ss_ready, 1)

            @block.scalar
            def _(act):
                act.wait_ge(loaded, total)
                nc.scalar.activation(sc[:], sc[:], ACT.Tanh).then_inc(scale_ready, 1)
                nc.scalar.activation(C["ident_bf"][:], C["ident"], ACT.Copy).then_inc(scale_ready, 1)
                with act.Fori(0, TILES // 2) as i:
                    act.wait_ge(h_ready, 2 * i + 1)
                    for k in range(2):
                        act.wait_ge(u_ready, 2 * i + k + 1)
                        nc.scalar.activation(sq[:, k, :], u[:, k, :], ACT.Square).then_inc(sq_ready, 1)
                    for k in range(2):
                        act.wait_ge(clamped, 2 * i + k + 1)
                        nc.scalar.activation(lg[:, k, :], lg[:, k, :], ACT.Ln).then_inc(log_ready, 1)
                    for k in range(2):
                        act.wait_ge(log_ready, 2 * i + k + 1)
                        nc.scalar.activation(nrm[:, k, :], lg[:, k, :], ACT.Exp, scale=0.5).then_inc(norm_ready, 1)
                        nc.scalar.activation(rn[:, k, :], lg[:, k, :], ACT.Exp, scale=-0.5).then_inc(norm_ready, 1)
                    for k in range(2):
                        act.wait_ge(norm_ready, 4 * i + 2 * k + 1)
                        nc.scalar.activation(f[:, k, :], nrm[:, k, :], ACT.Tanh).then_inc(tanh_ready, 1)

            @block.vector
            def _(dve):
                dve.wait_ge(loaded, total)
                dve.wait_ge(scale_ready, 1)
                dve.sem_inc(h_ready, 1)
                with dve.Fori(0, TILES // 2) as i:
                    dve.wait_ge(h_ready, 2 * i + 1)
                    for k in range(2):
                        dve.wait_ge(z_ready, 2 * i + k + 1)
                        nc.vector.tensor_scalar(u[:, k, :], ps[:, k, 0:TILE], b[:], sc[:], ALU.add, ALU.mult).then_inc(u_ready, 1)
                    for k in range(2):
                        dve.wait_ge(ss_ready, 2 * i + k + 1)
                        nc.vector.tensor_scalar(lg[:, k, :], ps[:, 2 + k, 0:TILE], float(D), 1e-18, ALU.mult, ALU.max).then_inc(clamped, 1)
                    for k in range(2):
                        dve.wait_ge(tanh_ready, 2 * i + k + 1)
                        nc.vector.scalar_tensor_tensor(f[:, k, :], f[:, k, :], BALL, rn[:, k, :], ALU.min, ALU.mult).then_inc(factor_ready, 1)
                        dve.wait_ge(factor_ready, 2 * i + k + 1)
                        nc.vector.tensor_tensor(hA[:, bass.ds(i * 2 * TILE + k * TILE, TILE)], u[:, k, :], f[:, k, :], ALU.mult).then_inc(h_ready, 1)
        sem.clear()


def stage_cross_attention(nc, io, hA, hn, ps, C):
    with ExitStack() as ctx:
        sb = lambda name, shape, dt=F32: ctx.enter_context(nc.sbuf_tensor(name, shape, dt))
        sem = Signals(nc, ctx)
        wq, wo = sb("xq_w", [P, P]), sb("xo_w", [P, GROUPS, P])
        bq, bk, bo, bv = sb("xq_b", [P, 1]), sb("xk_b", [P, 1]), sb("xo_b", [P, 1]), sb("xv_b", [P, GROUPS * P])
        kf, krest, kparts = sb("x_keys", [P, SRC]), sb("x_keys_rest", [P, SRC]), sb("x_key_parts", [P, 3, SRC], BF16)
        half = SRC // 2
        v = sb("x_values", [half, 2, GROUPS * P])
        ks = sb("x_key_stack", [6 * HD + 3, 1, HEADS, SRC], BF16)
        qs = sb("x_query_stack", [6 * HD + 3, 2, HEADS, TILE], BF16)
        xc, sq, rs, xn = sb("x_centered", [P, TILE]), sb("x_squares", [P, TILE]), sb("x_rstd", [P, TILE]), sb("x_normed", [P, TILE])
        xc2, sq2, rs2, hf = sb("x_centered2", [P, TILE]), sb("x_squares2", [P, TILE]), sb("x_rstd2", [P, TILE]), sb("x_normed2", [P, TILE])
        qf, qparts = sb("x_q", [P, TILE]), sb("x_q_parts", [P, 3, TILE], BF16)
        QB = 120
        NQ = TILE // QB
        mx, mparts = sb("x_max", [QB, NQ, HEADS]), sb("x_max_parts", [QB, NQ, 3, HEADS], BF16)
        mrows = sb("x_max_rows", [3 * HEADS, TILE], BF16)
        probs = sb("x_probs", [half, 3, 2, TILE])
        outs, rd = sb("x_outs", [P, GROUPS, TILE]), sb("x_rden", [P, GROUPS, TILE])
        on = rd
        loaded, k_sums, v_sums, v_ready, bias_ready = sem("x_loaded"), sem("x_k_sums"), sem("x_v_sums"), sem("x_v_ready"), sem("x_bias_ready")
        keys_loaded, minus_ready = sem("x_keys_loaded"), sem("x_minus_ready")
        zeros, zeros_ready = sb("x_zeros", [P, TILE]), sem("x_zeros_ready")
        keys = Split(nc, sem, "x_keys", kf[:], krest[:], kparts, io["scratch_k"][:, :, 0:SRC], K_ORDER, zeros[:, 0:SRC])
        flat = hn[:, :, :].rearrange("p a n -> p (a n)").bitcast(F32)
        sizes = [KC * P, KC * GROUPS * P, KC * SRC, KC * SRC]
        at0 = [sum(sizes[:n]) for n in range(4)]
        wk, wv, st, vt = [flat[:, a0:a0 + z].rearrange("p (c n) -> p c n", c=KC) for a0, z in zip(at0, sizes)]
        with nc.Block() as block:
            @block.sync
            def _(sp):
                n = load(sp, loaded, [(wk, io["x_WkT"]), (st, io["x_srcT"]), (wv, io["x_WvT"]), (vt, io["x_valT"]), (wq[:], io["x_Wq"]), (wo[:], io["x_Wo"]),
                                      (bq[:], io["x_bq"]), (bk[:], io["x_bk"]), (bo[:], io["x_bo"]), (bv[:], io["x_bv"].broadcast_to([P, GROUPS * P]))])
                sp.wait_ge(loaded, n)
                keys.sp(sp, 0, ks[:, 0], keys_loaded)
                sp.wait_ge(keys_loaded, 96)

            @block.tensor
            def _(pe):
                pe.wait_ge(loaded, 160)
                for c in range(KC):
                    last = nc.tensor.matmul(ps[:, 0, 0:SRC], wk[:, c, :], st[:, c, :], start=c == 0, stop=c == KC - 1)
                last.then_inc(k_sums, 1)
                for m in range(2):
                    for c in range(KC):
                        last = nc.tensor.matmul(ps[0:half, 2 + m, 0:GROUPS * P], vt[:, c, m * half:(m + 1) * half], wv[:, c, :], start=c == 0, stop=c == KC - 1)
                last.then_inc(v_sums, 1)

            @block.gpsimd
            def _(pool):
                nc.gpsimd.memset(ks[6 * HD:6 * HD + 3, 0], -1.0).then_inc(minus_ready, 1)
                pool.wait_ge(minus_ready, 1)
                nc.gpsimd.memset(zeros[:], 0.0).then_inc(zeros_ready, 1)
                pool.wait_ge(zeros_ready, 1)
                keys.pool(pool, 0)

            @block.vector
            def _(dve):
                dve.wait_ge(loaded, 160)
                dve.wait_ge(k_sums, 1)
                nc.vector.tensor_scalar(kf[:], ps[:, 0, 0:SRC], bk[:], None, ALU.add).then_inc(keys.full_ready, 1)
                nc.vector.tensor_tensor(bv[:], bv[:], C["ones_col"], ALU.add).then_inc(bias_ready, 1)
                dve.wait_ge(bias_ready, 1)
                dve.wait_ge(v_sums, 1)
                for m in range(2):
                    nc.vector.tensor_tensor(v[:, m, :], ps[0:half, 2 + m, 0:GROUPS * P], bv[0:half, :], ALU.add).then_inc(v_ready, 1)

        n1 = Norm(nc, sem, "x_n1", ps[:, 0, 0:TILE], ps[:, 1, 0:TILE], xc[:], sq[:], rs[:], C["ones"], C["eps"])
        n2 = Norm(nc, sem, "x_n2", ps[:, 7, 0:TILE], ps[:, 6, 0:TILE], xc2[:], sq2[:], rs2[:], C["ones"], C["eps"])
        queries = [(n * QB, QB, 0) for n in range(NQ)]
        units = [((2 * m, 2 * m + 1), 0, TILE, [(c * half, half, c, c == 0, c == 1)]) for m in range(HEADS // 2) for c in range(2)]
        at = Attention(nc, sem, "x_att", ps, TILE, queries, None, SRC, units, (qs, ks, mx, mparts, mrows, probs, outs, rd, on, C["sel"], C["ident_bf"]), C["eps"])
        at.turned = ps[0:3 * HEADS, 0, :].bitcast(BF16)[:, 0:TILE].rearrange("p (b n) -> p b n", n=QB)
        at.row_copies = [(mrows[:].rearrange("p (b n) -> p b n", n=QB), at.turned)]
        split = Split(nc, sem, "x_q", qf[:], xc[:], qparts, io["scratch_q"][:, :, 0:TILE], Q_ORDER, zeros[:])
        at.wait_stack = lambda pe, i: pe.wait_ge(at.stack_loaded, 96 * (i + 1))
        q_sums, proj_ready, h_ready, hi_ready, tile_done, rest_ready = sem("x_q_sums"), sem("x_proj_ready"), sem("x_h_ready"), sem("x_hi_ready"), sem("x_tile_done"), sem("x_rest_ready")
        tile = lambda i: bass.ds(i * TILE, TILE)
        values = lambda k, c: v[:, c, :]

        def started(eng, i):
            eng.wait_ge(tile_done, i + 1)
            eng.wait_ge(at.max_rows_loaded, 16 * (i + 1))

        def pe_front(pe, i, part):
            if part == 0:
                n1.pe_mean(hA[:, tile(i)])
                n1.pe_var(pe, i + 1)
                pe.wait_ge(n1.done, i + 1)
                nc.tensor.matmul(ps[:, 0, 0:TILE], wq[:], xn[:], start=True, stop=True).then_inc(q_sums, 1)

        def dve_front(dve, i):
            n1.dve(dve, i + 1, hA[:, tile(i)], xn[:])
            dve.wait_ge(q_sums, i + 1)
            nc.vector.tensor_scalar(qf[:], ps[:, 0, 0:TILE], bq[:], None, ALU.add).then_inc(split.full_ready, 1)
            for u in range(at.NM):
                at.dve_max(dve, i, u)
            at.dve_max_parts(dve, i)
            at.dve_rows(dve, i)

        def pe_step(pe, i, k, front):
            started(pe, i)
            at.pe_logits(pe, i, k, 0)
            at.pe_logits(pe, i, k, 1)
            if front:
                pe_front(pe, i + 1, 0)
            for u in range(2, at.NU):
                at.pe_values(pe, i, k, u - 2, values)
                at.pe_logits(pe, i, k, u)
                if front and u >= 5:
                    at.pe_scores(pe, i + 1, 1 - k, u - 5)
            for u in range(at.NU - 2, at.NU):
                at.pe_values(pe, i, k, u, values)
            if front:
                for u in range(3, 5):
                    at.pe_scores(pe, i + 1, 1 - k, u)
            at.pe_denominators(pe, i)
            pe.wait_ge(at.normed_ready, GROUPS * (i + 1))
            for g in range(GROUPS):
                last = nc.tensor.matmul(ps[:, 6, 0:TILE], wo[:, g, :], on[:, g, :], start=g == 0, stop=g == GROUPS - 1)
            last.then_inc(proj_ready, 1)
            if front:
                for u in range(5, at.NM):
                    at.pe_scores(pe, i + 1, 1 - k, u)
            pe.wait_ge(h_ready, i + 1)
            n2.pe_mean(hA[:, tile(i)])
            if front:
                at.pe_turn(pe, i + 1)
            n2.pe_var(pe, i + 1)

        def act_step(act, i, k, front):
            started(act, i)
            at.act_probs(act, i, 0)
            at.act_probs(act, i, 1)
            if front:
                n1.act(act, i + 2)
            for u in range(2, at.NU):
                at.act_probs(act, i, u)
            at.act_outs(act, i)
            n2.act(act, i + 1)

        def dve_step(dve, i, k, front):
            started(dve, i)
            if front:
                n1.dve(dve, i + 2, hA[:, tile(i + 1)], xn[:])
                dve.wait_ge(q_sums, i + 2)
                nc.vector.tensor_scalar(qf[:], ps[:, 0, 0:TILE], bq[:], None, ALU.add).then_inc(split.full_ready, 1)
                for u in range(5):
                    at.dve_max(dve, i + 1, u)
            at.dve_normed(dve, i)
            if front:
                for u in range(5, at.NM):
                    at.dve_max(dve, i + 1, u)
                at.dve_max_parts(dve, i + 1)
            dve.wait_ge(proj_ready, i + 1)
            nc.vector.scalar_tensor_tensor(hA[:, tile(i)], ps[:, 6, 0:TILE], bo[:], hA[:, tile(i)], ALU.add, ALU.add).then_inc(h_ready, 1)
            if front:
                at.dve_rows(dve, i + 1)
            dve.wait_ge(h_ready, i + 1)
            n2.dve(dve, i + 1, hA[:, tile(i)], hf[:])
            dve.wait_ge(n2.done, i + 1)
            nc.vector.tensor_copy(hn[:, 0, tile(i)], hf[:]).then_inc(hi_ready, 1)
            dve.wait_ge(hi_ready, i + 1)
            nc.vector.tensor_tensor(hn[:, 1, tile(i)], hf[:], hn[:, 0, tile(i)], ALU.subtract).then_inc(tile_done, 1)

        def in_pairs(eng, step):
            with eng.Fori(0, TILES // 2 - 1) as m:
                for k in range(2):
                    step(eng, 2 * m + k, k, True)
            step(eng, TILES - 2, 0, True)
            step(eng, TILES - 1, 1, False)

        with nc.Block() as block:
            @block.sync
            def _(sp):
                def step(sp, i, k, front):
                    if front:
                        split.sp(sp, i + 1, qs[:, 1 - k], at.stack_loaded)
                        at.sp_rows(sp, i + 1, 1 - k, io["scratch_m"][:, 0:TILE])
                split.sp(sp, 0, qs[:, 0], at.stack_loaded)
                at.sp_rows(sp, 0, 0, io["scratch_m"][:, 0:TILE])
                in_pairs(sp, step)

            @block.tensor
            def _(pe):
                pe_front(pe, 0, 0)
                for u in range(at.NM):
                    at.pe_scores(pe, 0, 0, u)
                at.pe_turn(pe, 0)
                in_pairs(pe, pe_step)

            @block.scalar
            def _(act):
                load_tables(nc, act, LN_EXP_SET)
                n1.act(act, 1)
                in_pairs(act, act_step)

            @block.gpsimd
            def _(pool):
                def step(pool, i, k, front):
                    started(pool, i)
                    if front:
                        split.pool(pool, i + 1)
                split.pool(pool, 0)
                in_pairs(pool, step)

            @block.vector
            def _(dve):
                dve.sem_inc(tile_done, 1)
                dve_front(dve, 0)
                in_pairs(dve, dve_step)
        sem.clear()


def stage_gru(nc, io, hA, hn, hB, ps, C):
    M = HID // P
    NB = BLOCK_STEPS * BATCH
    with ExitStack() as ctx:
        sb = lambda name, shape, dt=F32: ctx.enter_context(nc.sbuf_tensor(name, shape, dt))
        sem = Signals(nc, ctx)
        R, Z, CND, OUT = 0, 1, 2, 3
        wx, wh, wo = sb("gru_wx", [P, 2, 3, HID], F16), sb("gru_wh", [P, 2, M, 3, HID], F16), sb("gru_wo", [P, 2, M, P], F16)
        braw, bias = sb("gru_bias_raw", [P, 2, 3, P]), sb("gru_bias_parts", [P, 3, P], F16)
        brest, bp = sb("gru_bias_rest", [P, 3, P]), sb("gru_bias_part", [P, 3, P], F16)
        sel, bo = sb("gru_selector", [P, M * BATCH], F16), sb("gru_bo", [P, 1])
        h = sb("gru_h", [P, M * BATCH])
        hs = sb("gru_states", [P, 2, M, BLOCK_STEPS, BATCH], F16)
        r, z, c = sb("gru_r", [P, M * BATCH]), sb("gru_z", [P, M * BATCH]), sb("gru_c", [P, M * BATCH])
        rh, rhp = sb("gru_rh", [P, M * BATCH]), sb("gru_rh_parts", [P, 2, M, BATCH], F16)
        zh, omz, mc = sb("gru_zh", [P, M * BATCH]), sb("gru_omz", [P, M * BATCH]), sb("gru_mc", [P, M * BATCH])
        o = sb("gru_o", [P, NB])
        sizes = [3 * HID, M * 3 * HID, M * P]
        starts = [sum(sizes[:n]) for n in range(4)]
        stage = hB[:, 0:starts[3]]
        loaded, w_hi, w_lo, bias_step, cleared, ready = sem("gru_loaded"), sem("gru_w_hi"), sem("gru_w_lo"), sem("gru_bias_step"), sem("gru_cleared"), sem("gru_ready")
        flats = [wx[:].rearrange("p a g n -> p a (g n)"), wh[:].rearrange("p a m g n -> p a (m g n)"), wo[:].rearrange("p a m n -> p a (m n)")]
        with nc.Block() as block:
            @block.gpsimd
            def _(pool):
                nc.gpsimd.memset(braw[:], 0.0).then_inc(cleared, 1)
                pool.wait_ge(cleared, 1)
                nc.gpsimd.memset(hs[:], 0.0).then_inc(cleared, 1)
                pool.wait_ge(cleared, 2)
                nc.gpsimd.memset(h[:], 0.0).then_inc(cleared, 1)
                pool.wait_ge(cleared, 3)
                nc.gpsimd.memset(bias[:], 0.0).then_inc(cleared, 1)

            @block.sync
            def _(sp):
                load(sp, loaded, [(stage[:, starts[0]:starts[1]], io["g_Wx"]), (stage[:, starts[1]:starts[2]], io["g_Wh"]),
                                  (stage[:, starts[2]:starts[3]], io["g_Wo"]), (bo[:], io["g_bo"]), (r[:], io["g_sel"])])
                sp.wait_ge(cleared, 4)
                load(sp, loaded, [(braw[SLOT * p:SLOT * p + M, s], io["g_b"][:, s]) for p in range(3) for s in range(2)])
                sp.wait_ge(loaded, 176)

            @block.vector
            def _(dve):
                v = nc.vector
                dve.wait_ge(loaded, 176)
                for n, f in enumerate(flats):
                    src = stage[:, starts[n]:starts[n + 1]]
                    v.tensor_copy(f[:, 0, :], src).then_inc(w_hi, 1)
                    dve.wait_ge(w_hi, n + 1)
                    v.tensor_tensor(f[:, 1, :], src, f[:, 0, :], ALU.subtract).then_inc(w_lo, 1)
                v.tensor_copy(sel[:], r[:]).then_inc(bias_step, 1)
                dve.wait_ge(bias_step, 1)
                v.tensor_tensor(brest[:], braw[:, 0], braw[:, 1], ALU.add).then_inc(bias_step, 1)
                for p in range(3):
                    dve.wait_ge(bias_step, 2 + 3 * p)
                    v.tensor_copy(bp[:], brest[:]).then_inc(bias_step, 1)
                    dve.wait_ge(bias_step, 3 + 3 * p)
                    v.tensor_copy(bias[SLOT * p:SLOT * p + M], bp[SLOT * p:SLOT * p + M]).then_inc(bias_step, 1)
                    v.tensor_tensor(brest[:], brest[:], bp[:], ALU.subtract).then_inc(bias_step, 1)
                dve.wait_ge(w_lo, 3)

        x_sums = [sem(f"gru_x_sums{g}") for g in range(3)]
        sums = [sem(f"gru_sums{g}") for g in range(3)]
        r_ready, z_ready, c_ready = sem("gru_r_ready"), sem("gru_z_ready"), sem("gru_c_ready")
        rh_hi, rh_full, rh_lo = sem("gru_rh_hi"), sem("gru_rh_full"), sem("gru_rh_lo")
        zh_ready, omz_ready, mc_ready = sem("gru_zh_ready"), sem("gru_omz_ready"), sem("gru_mc_ready")
        h_hi, h_full, h_lo = sem("gru_h_hi"), sem("gru_h_full"), sem("gru_h_lo")
        out_sums, o_ready, out_done = sem("gru_out_sums"), sem("gru_o_ready"), sem("gru_out_done")
        bank = lambda g, m: ps[:, g, m * BATCH:(m + 1) * BATCH]
        hview = hs[:]

        def x_products(t, g):
            nc.tensor.matmul(ps[:, g, 0:M * BATCH], bias[:, g, :], sel[:], start=True, stop=False, skip_group_check=True)
            for m in range(M):
                for a, b in ((0, 0), (0, 1), (1, 0)):
                    nc.tensor.matmul(bank(g, m), wx[:, a, g, m * P:(m + 1) * P], hn[:, b, bass.ds(t * BATCH, BATCH)],
                                     start=False, stop=False, skip_group_check=True)

        def h_products(pe, g, state, lo_sem, lo_value):
            for a in (0, 1):
                for m in range(M):
                    for k in range(M):
                        nc.tensor.matmul(bank(g, m), wh[:, a, k, g, m * P:(m + 1) * P], state(0, k), start=False, stop=False, skip_group_check=True)
            pe.wait_ge(lo_sem, lo_value)
            for m in range(M):
                for k in range(M):
                    last = nc.tensor.matmul(bank(g, m), wh[:, 0, k, g, m * P:(m + 1) * P], state(1, k), start=False,
                                            stop=m == M - 1 and k == M - 1, skip_group_check=True)
            last.then_inc(sums[g], 1)

        def per_step(eng, body):
            with eng.Fori(0, STEPS // BLOCK_STEPS) as i:
                for s in range(BLOCK_STEPS):
                    body(i * BLOCK_STEPS + s, i, s)

        def block_end(pe, i, more):
            t = i * BLOCK_STEPS + BLOCK_STEPS
            if more:
                x_products(t, R)
                pe.wait_ge(z_ready, t)
                x_products(t, Z)
                pe.wait_ge(c_ready, t)
                x_products(t, CND)
            pe.wait_ge(h_lo, t + 1)
            pe.wait_ge(out_done, i + 1)
            n = 0
            for a, b in ((0, 0), (1, 0), (0, 1)):
                for k in range(M):
                    last = nc.tensor.matmul(ps[:, OUT, 0:NB], wo[:, a, k, :], hview[:, b, k].rearrange("p s b -> p (s b)"), start=n == 0, stop=n == 3 * M - 1)
                    n += 1
            last.then_inc(out_sums, 1)

        with nc.Block() as block:
            @block.tensor
            def _(pe):
                for g in range(3):
                    x_products(0, g)

                def body(t, i, s):
                    prev = (s - 1) % BLOCK_STEPS
                    old = lambda part, k: hview[:, part, k, prev, :]
                    pe.wait_ge(h_hi, t + 1)
                    h_products(pe, R, old, h_lo, t + 1)
                    h_products(pe, Z, old, h_lo, t + 1)
                    pe.wait_ge(r_ready, t + 1)
                    if s < BLOCK_STEPS - 1:
                        x_products(t + 1, R)
                    pe.wait_ge(rh_hi, t + 1)
                    h_products(pe, CND, lambda part, k: rhp[:, part, k, :], rh_lo, t + 1)
                    if s < BLOCK_STEPS - 1:
                        pe.wait_ge(z_ready, t + 1)
                        x_products(t + 1, Z)
                        pe.wait_ge(c_ready, t + 1)
                        x_products(t + 1, CND)

                with pe.Fori(0, STEPS // BLOCK_STEPS - 1) as i:
                    for s in range(BLOCK_STEPS):
                        body(i * BLOCK_STEPS + s, i, s)
                    block_end(pe, i, True)
                i = STEPS // BLOCK_STEPS - 1
                for s in range(BLOCK_STEPS):
                    body(i * BLOCK_STEPS + s, i, s)
                block_end(pe, i, False)

            @block.scalar
            def _(act):
                def body(t, i, s):
                    act.wait_ge(sums[R], t + 1)
                    nc.scalar.activation(r[:], ps[:, R, 0:M * BATCH], ACT.Sigmoid).then_inc(r_ready, 1)
                    act.wait_ge(sums[Z], t + 1)
                    nc.scalar.activation(z[:], ps[:, Z, 0:M * BATCH], ACT.Sigmoid).then_inc(z_ready, 1)
                    act.wait_ge(sums[CND], t + 1)
                    nc.scalar.activation(c[:], ps[:, CND, 0:M * BATCH], ACT.Tanh).then_inc(c_ready, 1)
                load_tables(nc, act, SIGMOID_SET)
                with act.Fori(0, STEPS // BLOCK_STEPS) as i:
                    for s in range(BLOCK_STEPS):
                        body(i * BLOCK_STEPS + s, i, s)
                    act.wait_ge(out_sums, i + 1)
                    nc.scalar.activation(o[:], ps[:, OUT, 0:NB], ACT.Sigmoid, bias=bo[:]).then_inc(o_ready, 1)

            @block.gpsimd
            def _(pool):
                with pool.Fori(0, STEPS // BLOCK_STEPS) as i:
                    for s in range(BLOCK_STEPS):
                        t = i * BLOCK_STEPS + s
                        pool.wait_ge(h_full, t + 1)
                        pool.wait_ge(z_ready, t + 1)
                        nc.gpsimd.tensor_tensor(zh[:], z[:], h[:], ALU.mult).then_inc(zh_ready, 1)

            @block.vector
            def _(dve):
                v = nc.vector
                dve.sem_inc(h_hi, 1)
                dve.sem_inc(h_full, 1)
                dve.sem_inc(h_lo, 1)
                dve.sem_inc(out_done, 1)
                with dve.Fori(0, STEPS // BLOCK_STEPS) as i:
                    for s in range(BLOCK_STEPS):
                        t = i * BLOCK_STEPS + s
                        flat = lambda x: x.rearrange("p k b -> p (k b)")
                        dve.wait_ge(r_ready, t + 1)
                        dve.wait_ge(h_lo, t + 1)
                        v.tensor_tensor(flat(rhp[:, 0]), r[:], h[:], ALU.mult).then_inc(rh_hi, 1)
                        v.tensor_tensor(rh[:], r[:], h[:], ALU.mult).then_inc(rh_full, 1)
                        dve.wait_ge(rh_full, t + 1)
                        v.tensor_tensor(flat(rhp[:, 1]), rh[:], flat(rhp[:, 0]), ALU.subtract).then_inc(rh_lo, 1)
                        dve.wait_ge(z_ready, t + 1)
                        v.tensor_scalar(omz[:], z[:], -1.0, 1.0, ALU.mult, ALU.add).then_inc(omz_ready, 1)
                        dve.wait_ge(omz_ready, t + 1)
                        dve.wait_ge(c_ready, t + 1)
                        v.tensor_tensor(mc[:], omz[:], c[:], ALU.mult).then_inc(mc_ready, 1)
                        dve.wait_ge(mc_ready, t + 1)
                        dve.wait_ge(zh_ready, t + 1)
                        split = lambda x: x[:].rearrange("p (k b) -> p k b", k=M)
                        v.tensor_tensor(hview[:, 0, :, s, :], split(mc), split(zh), ALU.add).then_inc(h_hi, 1)
                        v.tensor_tensor(h[:], mc[:], zh[:], ALU.add).then_inc(h_full, 1)
                        dve.wait_ge(h_full, t + 2)
                        v.tensor_tensor(hview[:, 1, :, s, :], split(h), hview[:, 0, :, s, :], ALU.subtract).then_inc(h_lo, 1)
                    dve.wait_ge(o_ready, i + 1)
                    src = lambda x: x.rearrange("p (s b) -> p b s", b=BATCH)
                    dst = hB[:, :].rearrange("p (b s) -> p b s", s=STEPS)[:, :, bass.ds(i * BLOCK_STEPS, BLOCK_STEPS)]
                    v.tensor_tensor(dst, src(o[:]), src(hA[:, bass.ds(i * NB, NB)]), ALU.add).then_inc(out_done, 1)
        sem.clear()


def stage_self_attention(nc, io, hB, ps, C):
    W = 2 * STEPS
    NT = BATCH // 2
    KN = (STEPS + 1) // 2
    OV = STEPS - KN
    FC = DFF // P
    with ExitStack() as ctx:
        sb = lambda name, shape, dt=F32: ctx.enter_context(nc.sbuf_tensor(name, shape, dt))
        sem = Signals(nc, ctx)
        wqk, wv, wo = sb("s_wqk", [P, 4, P]), sb("s_wv", [P, GROUPS * P]), sb("s_wo", [P, GROUPS, P])
        w1, w2 = sb("s_w1", [P, FC, P]), sb("s_w2", [P, FC, P])
        cols = sb("s_columns", [P, FC + 5])
        b1, (b2, g1, be1, g2, be2) = cols[:, 0:FC], [cols[:, FC + n:FC + n + 1] for n in range(5)]
        rope = sb("s_rope", [P, 2, W])
        vmask, vpat = sb("s_value_mask", [KN, 2]), sb("s_value_pattern", [KN, 2, 2 * GROUPS * P])
        ks, qs = sb("s_key_stack", [6 * HD + 3, 2, HEADS, W], BF16), sb("s_query_stack", [6 * HD + 3, 2, HEADS, W], BF16)
        xn, v = sb("s_normed", [P, 2, W]), sb("s_values", [KN, 2, 4, GROUPS * P])
        lns = [[sb(f"s_{n}{m}", [P, W]) for n in ("centered", "squares", "rstd")] for m in range(3)]
        t1, t2, qf, kf, rest = sb("s_t1", [P, W]), sb("s_t2", [P, W]), sb("s_q", [P, W]), sb("s_k", [P, W]), sb("s_rest", [P, W])
        qparts, kparts, zeros = sb("s_q_parts", [P, 3, W], BF16), sb("s_k_parts", [P, 3, W], BF16), sb("s_zeros", [P, W])
        mx, mparts = sb("s_max", [KN, 4, HEADS]), sb("s_max_parts", [KN, 4, 3, HEADS], BF16)
        mrows = sb("s_max_rows", [3 * HEADS, W], BF16)
        probs = sb("s_probs", [KN, 3, 2, 2 * STEPS])
        outs, rd = sb("s_outs", [P, GROUPS, W]), sb("s_rden", [P, GROUPS, W])
        x1, x2, hid = sb("s_x1", [P, W]), sb("s_x2", [P, W]), sb("s_hidden", [P, FC, W])
        loaded, cleared = sem("s_loaded"), sem("s_cleared")
        queries = [(b * STEPS + c * OV, KN, b * STEPS) for b in range(2) for c in range(2)]
        units = [((2 * m, 2 * m + 1), b * STEPS, STEPS,
                  [(b * STEPS + c * OV, KN, 2 * b + c, c == 0, c == 1) for c in range(2)]) for m in range(HEADS // 2) for b in range(2)]
        at = Attention(nc, sem, "s_att", ps, W, queries, None, STEPS, units, (qs, ks, mx, mparts, mrows, probs, outs, rd, rd, C["sel"], C["ident_bf"]), C["eps"])
        pitch = KN + KN % 2 + 2 * (KN % 2 == 0)
        at.turned = ps[0:3 * HEADS, 0, :].bitcast(BF16)[:, 0:4 * pitch].rearrange("p (b n) -> p b n", n=pitch)
        rows = mrows[:].rearrange("p (b n) -> p b n", n=STEPS)
        at.row_copies = [(rows[:, :, 0:KN], at.turned[:, 0::2, 0:KN]), (rows[:, :, KN:STEPS], at.turned[:, 1::2, KN - OV:KN])]
        at.wait_stack = lambda pe, i: pe.wait_ge(at.stack_loaded, 192 * (i + 1))
        n0 = Norm(nc, sem, "s_n0", ps[:, 0, 0:W], ps[:, 1, 0:W], *[x[:] for x in lns[0]], C["ones"], C["eps"])
        n1 = Norm(nc, sem, "s_n1", ps[:, 7, 0:W], ps[:, 6, 0:W], *[x[:] for x in lns[1]], C["ones"], C["eps"])
        n2 = Norm(nc, sem, "s_n2", ps[:, 7, 0:W], ps[:, 6, 0:W], *[x[:] for x in lns[2]], C["ones"], C["eps"])
        qsplit = Split(nc, sem, "s_q", qf[:], rest[:], qparts, io["scratch_q"][:, :, 0:W], Q_ORDER, zeros[:])
        ksplit = Split(nc, sem, "s_k", kf[:], rest[:], kparts, io["scratch_k"][:, :, 0:W], K_ORDER, zeros[:])
        qk_sums, turned_ready = [sem(f"s_qk_sums{n}") for n in range(2)], sem("s_turned_ready")
        v_sums, v_ready, proj_ready, x1_in, x1_ready = sem("s_v_sums"), sem("s_v_ready"), sem("s_proj_ready"), sem("s_x1_in"), sem("s_x1_ready")
        hid_sums, hid_ready, ffn_sums, x2_in, y_ready, tile_done = sem("s_hidden_sums"), sem("s_hidden_ready"), sem("s_ffn_sums"), sem("s_x2_in"), sem("s_y_ready"), sem("s_tile_done")
        tile = lambda i: bass.ds(i * W, W)
        values = lambda k, n: v[:, k, n, :]

        def started(eng, i):
            eng.wait_ge(tile_done, i + 1)
            eng.wait_ge(at.max_rows_loaded, 16 * (i + 1))

        def pe_front(pe, i, k):
            n0.pe_mean(hB[:, tile(i)])
            n0.pe_var(pe, i + 1)
            pe.wait_ge(n0.done, i + 1)
            for n in range(2):
                if n == 1:
                    pe.wait_ge(turned_ready, 4 * i + 2)
                for m in range(2):
                    last = nc.tensor.matmul(ps[:, m, 0:W], wqk[:, 2 * n + m, :], xn[:, k, :], start=True, stop=True)
                last.then_inc(qk_sums[n], 1)
            pe.wait_ge(turned_ready, 4 * i + 4)
            for c in range(2):
                for b in range(2):
                    last = nc.tensor.matmul(ps[0:KN, c, b * GROUPS * P:(b + 1) * GROUPS * P], xn[:, k, b * STEPS + c * OV:b * STEPS + c * OV + KN], wv[:], start=True, stop=True)
                last.then_inc(v_sums, 1)

        def dve_front(dve, i, k):
            vec = nc.vector
            n0.dve(dve, i + 1, hB[:, tile(i)], xn[:, k, :])
            for n, (full, split) in enumerate(((qf, qsplit), (kf, ksplit))):
                dve.wait_ge(qk_sums[n], i + 1)
                if n == 1:
                    dve.wait_ge(qsplit.full_ready, i + 1)
                vec.tensor_tensor(t1[:], ps[:, 0, 0:W], rope[:, 0, :], ALU.mult).then_inc(turned_ready, 1)
                vec.tensor_tensor(t2[:], ps[:, 1, 0:W], rope[:, 1, :], ALU.mult).then_inc(turned_ready, 1)
                dve.wait_ge(turned_ready, 4 * i + 2 * n + 2)
                vec.tensor_tensor(full[:], t1[:], t2[:], ALU.add).then_inc(split.full_ready, 1)
            for c in range(2):
                dve.wait_ge(v_sums, 2 * i + c + 1)
                vec.scalar_tensor_tensor(v[:, k, c::2, :], ps[0:KN, c, :].rearrange("p (b n) -> p b n", b=2), vmask[:, c:c + 1],
                                         vpat[:, c, :].rearrange("p (b n) -> p b n", b=2), ALU.mult, ALU.add).then_inc(v_ready, 1)

        def pe_scores(pe, i, k, us):
            for u in us:
                if u == 0:
                    pe.wait_ge(v_ready, 2 * (i + 1))
                at.pe_scores(pe, i, k, u)

        def pe_step(pe, i, k, front):
            started(pe, i)
            at.pe_logits(pe, i, k, 0)
            at.pe_logits(pe, i, k, 1)
            for u in range(2, at.NU):
                at.pe_values(pe, i, k, u - 2, values)
                at.pe_logits(pe, i, k, u)
                if front and u == 3:
                    pe_front(pe, i + 1, 1 - k)
            for u in range(at.NU - 2, at.NU):
                at.pe_values(pe, i, k, u, values)
            at.pe_denominators(pe, i)
            if front:
                pe_scores(pe, i + 1, 1 - k, range(0, 2))
            pe.wait_ge(at.normed_ready, GROUPS * (i + 1))
            for g in range(GROUPS):
                last = nc.tensor.matmul(ps[:, 6, 0:W], wo[:, g, :], rd[:, g, :], start=g == 0, stop=g == GROUPS - 1)
            last.then_inc(proj_ready, 1)
            if front:
                pe_scores(pe, i + 1, 1 - k, range(2, 4))
            pe.wait_ge(x1_in, i + 1)
            n1.pe_mean(x2[:])
            if front:
                pe_scores(pe, i + 1, 1 - k, range(4, 6))
            n1.pe_var(pe, i + 1)
            if front:
                pe_scores(pe, i + 1, 1 - k, range(6, 8))
            pe.wait_ge(x1_ready, i + 1)
            for m in range(FC):
                nc.tensor.matmul(ps[:, 2 + m, 0:W], w1[:, m, :], x1[:], start=True, stop=True).then_inc(hid_sums, 1)
            for m in range(FC):
                pe.wait_ge(hid_ready, FC * i + m + 1)
                last = nc.tensor.matmul(ps[:, 6, 0:W], w2[:, m, :], hid[:, m, :], start=m == 0, stop=m == FC - 1)
            last.then_inc(ffn_sums, 1)
            if front:
                at.pe_turn(pe, i + 1)
            pe.wait_ge(x2_in, i + 1)
            n2.pe_mean(x2[:])
            n2.pe_var(pe, i + 1)

        def act_step(act, i, k, front):
            started(act, i)
            for u in range(at.NU):
                at.act_probs(act, i, u)
                if front and u == 3:
                    n0.act(act, i + 2)
            at.act_outs(act, i)
            n1.act(act, i + 1)
            for m in range(FC):
                act.wait_ge(hid_sums, FC * i + m + 1)
                nc.scalar.activation(hid[:, m, :], ps[:, 2 + m, 0:W], ACT.Relu, bias=b1[:, m:m + 1]).then_inc(hid_ready, 1)
            n2.act(act, i + 1)

        def dve_step(dve, i, k, front):
            vec = nc.vector
            started(dve, i)
            if front:
                dve_front(dve, i + 1, 1 - k)
                for u in range(2):
                    at.dve_max(dve, i + 1, u)
            at.dve_normed(dve, i)
            if front:
                for u in range(2, 4):
                    at.dve_max(dve, i + 1, u)
            dve.wait_ge(proj_ready, i + 1)
            vec.tensor_tensor(x2[:], ps[:, 6, 0:W], xn[:, k, :], ALU.add).then_inc(x1_in, 1)
            dve.wait_ge(x1_in, i + 1)
            n1.dve_center(dve, i + 1, x2[:])
            if front:
                for u in range(4, 6):
                    at.dve_max(dve, i + 1, u)
            n1.dve_scale(dve, i + 1, x1[:])
            dve.wait_ge(n1.done, i + 1)
            vec.tensor_scalar(x1[:], x1[:], g1, be1, ALU.mult, ALU.add).then_inc(x1_ready, 1)
            if front:
                for u in range(6, 8):
                    at.dve_max(dve, i + 1, u)
                at.dve_max_parts(dve, i + 1)
            dve.wait_ge(ffn_sums, i + 1)
            vec.scalar_tensor_tensor(x2[:], ps[:, 6, 0:W], b2, x1[:], ALU.add, ALU.add).then_inc(x2_in, 1)
            if front:
                at.dve_rows(dve, i + 1)
            dve.wait_ge(x2_in, i + 1)
            n2.dve(dve, i + 1, x2[:], x1[:])
            dve.wait_ge(n2.done, i + 1)
            vec.tensor_scalar(x1[:], x1[:], g2, be2, ALU.mult, ALU.add).then_inc(y_ready, 1)
            dve.wait_ge(y_ready, i + 1)
            vec.tensor_tensor(hB[:, tile(i)], hB[:, tile(i)], x1[:], ALU.add).then_inc(tile_done, 1)

        def in_pairs(eng, step):
            with eng.Fori(0, NT // 2 - 1) as m:
                for k in range(2):
                    step(eng, 2 * m + k, k, True)
            step(eng, NT - 2, 0, True)
            step(eng, NT - 1, 1, False)

        with nc.Block() as block:
            @block.sync
            def _(sp):
                n = load(sp, loaded, [(wqk[:], io["s_wqk"]), (wv[:], io["s_wv"]), (wo[:], io["s_wo"]), (w1[:], io["s_w1"]), (w2[:], io["s_w2"]),
                                      (cols[:], io["s_columns"]), (rope[:], io["s_rope"]), (vmask[:], io["s_vmask"]), (vpat[:], io["s_vpat"])])
                sp.wait_ge(loaded, n)

            @block.gpsimd
            def _(pool):
                nc.gpsimd.memset(ks[6 * HD:6 * HD + 3], -1.0).then_inc(cleared, 1)
                pool.wait_ge(cleared, 1)
                nc.gpsimd.memset(zeros[:], 0.0).then_inc(cleared, 1)

        with nc.Block() as block:
            @block.sync
            def _(sp):
                def fill(sp, i, k):
                    qsplit.sp(sp, i, qs[:, k], at.stack_loaded)
                    ksplit.sp(sp, i, ks[:, k], at.stack_loaded)
                    at.sp_rows(sp, i, k, io["scratch_m"][:, 0:W])

                def step(sp, i, k, front):
                    if front:
                        fill(sp, i + 1, 1 - k)
                fill(sp, 0, 0)
                in_pairs(sp, step)

            @block.tensor
            def _(pe):
                pe_front(pe, 0, 0)
                pe_scores(pe, 0, 0, range(at.NM))
                at.pe_turn(pe, 0)
                in_pairs(pe, pe_step)

            @block.scalar
            def _(act):
                load_tables(nc, act, LN_EXP_SET)
                n0.act(act, 1)
                in_pairs(act, act_step)

            @block.gpsimd
            def _(pool):
                def splits(pool, i):
                    qsplit.pool(pool, i)
                    pool.wait_ge(qsplit.part_ready, 3 * (i + 1))
                    ksplit.pool(pool, i)

                def step(pool, i, k, front):
                    started(pool, i)
                    if front:
                        splits(pool, i + 1)
                splits(pool, 0)
                in_pairs(pool, step)

            @block.vector
            def _(dve):
                dve.sem_inc(tile_done, 1)
                dve_front(dve, 0, 0)
                for u in range(at.NM):
                    at.dve_max(dve, 0, u)
                at.dve_max_parts(dve, 0)
                at.dve_rows(dve, 0)
                in_pairs(dve, dve_step)
        sem.clear()


def stage_experts(nc, io, out, hB, ps, C):
    E1 = EXPERTS + 1
    QB = 120
    NQ = TILE // QB
    with ExitStack() as ctx:
        sb = lambda name, shape, dt=F32: ctx.enter_context(nc.sbuf_tensor(name, shape, dt))
        sem = Signals(nc, ctx)
        w1, w2 = sb("e_w1", [P, E1, 2, INTER]), sb("e_w2", [INTER, E1, P])
        gw, gb, rank = sb("e_gate_w", [P, EXPERTS]), sb("e_gate_b", [QB, NQ, EXPERTS]), sb("e_rank", [QB, NQ, EXPERTS])
        b1 = sb("e_b1", [INTER, 2, E1])
        acts = sb("e_act", [INTER, 5, E1])
        b2, b2s = sb("e_b2", [P, P]), sb("e_b2_shared", [P, 1])
        clamp, tmp = sb("e_clamp", [INTER, 2, E1]), sb("e_tmp", [INTER, 2, E1])
        lo, hi = sb("e_lo", [INTER, 2, E1]), sb("e_hi", [INTER, 2, E1])
        abias, ushift = sb("e_alpha_bias", [INTER, E1]), sb("e_up_shift", [INTER, E1])
        xn = sb("e_normed", [P, 2, TILE])
        xc, sq, rs = sb("e_centered", [P, TILE]), sb("e_squares", [P, TILE]), sb("e_rstd", [P, TILE])
        small = lambda name: sb(name, [QB, NQ, EXPERTS])
        logits, same, score, first, masked, second, cw = [small("e_" + n) for n in ("logits", "same", "score", "first", "masked", "second", "weights")]
        top = lambda name: sb(name, [QB, NQ, 1])
        m1, s1, m2, s2, gap, p1, p2 = [top("e_" + n) for n in ("max1", "score1", "max2", "score2", "gap", "p1", "p2")]
        cwT = sb("e_weight_rows", [P, TILE])
        cwb = sb("e_weights_everywhere", [INTER, 2, EXPERTS, TILE])
        g0, u0, sg, tt, t2, t3 = [sb("e_" + n, [INTER, 2, TILE]) for n in ("gate", "up", "sigmoid", "gated", "product", "weighted")]
        y = sb("e_out", [P, 2, TILE])
        loaded, prep, act_prep, cleared = sem("e_loaded"), sem("e_prep"), sem("e_act_prep"), sem("e_cleared")
        with nc.Block() as block:
            @block.gpsimd
            def _(pool):
                nc.gpsimd.memset(cwT[:], 0.0).then_inc(cleared, 1)

            @block.sync
            def _(sp):
                n = load(sp, loaded, [(w1[:], io["e_w1"]), (w2[:], io["e_w2"]), (gw[:], io["e_gate_w"]), (gb[:], io["e_gate_b"].broadcast_to([QB, NQ, EXPERTS])),
                                      (rank[:], io["e_rank"].broadcast_to([QB, NQ, EXPERTS])), (b1[:], io["e_b1"]),
                                      (acts[:], io["e_act"].broadcast_to([INTER, 5, E1])), (b2[:], io["e_b2"]), (b2s[:], io["e_b2s"])])
                assert n == 144
                sp.wait_ge(loaded, n)

            @block.scalar
            def _(act):
                load_tables(nc, act, LN_EXP_SET)
                act.wait_ge(prep, 2)
                nc.scalar.activation(tmp[:], tmp[:], ACT.Exp, scale=-1.0).then_inc(act_prep, 1)
                act.wait_ge(prep, 3)
                nc.scalar.activation(tmp[:], tmp[:], ACT.Ln).then_inc(act_prep, 1)

            @block.vector
            def _(dve):
                v = nc.vector
                done = [0]

                def then(instruction):
                    done[0] += 1
                    instruction.then_inc(prep, 1)
                    dve.wait_ge(prep, done[0])

                dve.wait_ge(loaded, 144)
                raw = acts[:, 3:5, :]
                then(v.tensor_scalar(tmp[:], raw, -1.0, None, ALU.mult))
                then(v.tensor_tensor(tmp[:], tmp[:], raw, ALU.max))
                dve.wait_ge(act_prep, 1)
                then(v.tensor_scalar(tmp[:], tmp[:], 1.0, None, ALU.add))
                dve.wait_ge(act_prep, 2)
                then(v.scalar_tensor_tensor(clamp[:], raw, 0.0, tmp[:], ALU.max, ALU.add))
                then(v.tensor_tensor(hi[:], clamp[:], b1[:], ALU.subtract))
                then(v.scalar_tensor_tensor(lo[:], clamp[:], -1.0, b1[:], ALU.mult, ALU.subtract))
                then(v.tensor_tensor(abias[:], acts[:, 0, :], b1[:, 0, :], ALU.mult))
                then(v.tensor_tensor(ushift[:], acts[:, 2, :], b1[:, 1, :], ALU.add))
                for e in range(E1):
                    then(v.tensor_scalar(w2[:, e, :], w2[:, e, :], acts[:, 1, e:e + 1], None, ALU.mult))

        n0 = Norm(nc, sem, "e_n0", ps[:, 6, 0:TILE], ps[:, 7, 0:TILE], xc[:], sq[:], rs[:], C["ones"], C["eps"])
        gate_sums, route, gap_ready, top_ready, rows_sums, rows_ready, rows_kept, rows_loaded = [
            sem("e_" + n) for n in ("gate_sums", "route", "gap_ready", "top_weights", "row_sums", "rows_ready", "rows_kept", "rows_loaded")]
        h_sums, g_ready, u_ready, s_ready, gated_ready, product_ready, weighted_ready, used = [
            sem("e_" + n) for n in ("h_sums", "g_ready", "u_ready", "s_ready", "gated_ready", "product_ready", "weighted_ready", "used")]
        y_ready = sem("e_y_ready")
        LOGITS = ps[0:QB, 5, 0:NQ * EXPERTS].rearrange("p (b e) -> p b e", e=EXPERTS)
        tile = lambda i: bass.ds(i * TILE, TILE)
        wide = lambda x: x[:].broadcast_to([QB, NQ, EXPERTS])
        NR = 15

        def started(eng, i):
            eng.wait_ge(y_ready, i + 1)
            eng.wait_ge(rows_loaded, 16 * (i + 1))

        def pe_gate(pe, i, k):
            pe.wait_ge(n0.done, i + 1)
            for b in range(NQ):
                last = nc.tensor.matmul(LOGITS[:, b, :], xn[:, k, b * QB:(b + 1) * QB], gw[:], start=True, stop=True)
            last.then_inc(gate_sums, 1)

        def pe_rows(pe, i):
            pe.wait_ge(route, NR * (i + 1))
            for b in range(NQ):
                last = nc.tensor.transpose(ps[0:EXPERTS, 5, b * QB:(b + 1) * QB], cw[:, b, :], C["ident"][0:QB, 0:QB])
            last.then_inc(rows_sums, 1)

        def routing_chain(dve, i, steps):
            def then(instruction):
                steps[0] += 1
                instruction.then_inc(route, 1)
                dve.wait_ge(route, NR * i + steps[0])
            return then

        def dve_choose(dve, i):
            v = nc.vector
            steps = [0]
            then = routing_chain(dve, i, steps)
            dve.wait_ge(gate_sums, i + 1)
            then(v.tensor_tensor(logits[:], LOGITS, gb[:], ALU.add))
            for values, best, scored, chosen in ((logits, m1, s1, first), (masked, m2, s2, second)):
                then(v.tensor_reduce(best[:], values[:], AX.X, ALU.max))
                then(v.tensor_tensor(same[:], values[:], wide(best), ALU.is_equal))
                then(v.tensor_tensor(score[:], same[:], rank[:], ALU.mult))
                then(v.tensor_reduce(scored[:], score[:], AX.X, ALU.max))
                then(v.tensor_tensor(chosen[:], score[:], wide(scored), ALU.is_equal))
                if chosen is first:
                    then(v.scalar_tensor_tensor(masked[:], first[:], -3e38, logits[:], ALU.mult, ALU.add))
            assert steps[0] == NR - 3
            v.tensor_tensor(gap[:], m2[:], m1[:], ALU.subtract).then_inc(gap_ready, 1)

        def dve_weigh(dve, i):
            v = nc.vector
            then = routing_chain(dve, i, [NR - 3])
            dve.wait_ge(top_ready, 2 * (i + 1))
            then(v.tensor_tensor(first[:], first[:], wide(p1), ALU.mult))
            then(v.tensor_tensor(second[:], second[:], wide(p2), ALU.mult))
            then(v.tensor_tensor(cw[:], first[:], second[:], ALU.add))

        def act_route(act, i):
            act.wait_ge(gap_ready, i + 1)
            nc.scalar.activation(p1[:], gap[:], ACT.Sigmoid, scale=-1.0).then_inc(top_ready, 1)
            nc.scalar.activation(p2[:], gap[:], ACT.Sigmoid).then_inc(top_ready, 1)

        def dve_rows(dve, i):
            dve.wait_ge(rows_sums, i + 1)
            nc.vector.tensor_copy(cwT[0:EXPERTS, :], ps[0:EXPERTS, 5, 0:TILE]).then_inc(rows_ready, 1)

        def sp_rows(sp, i, k):
            sp.wait_ge(rows_ready, i + 1)
            sp.dma_start(io["scratch_w"], cwT[0:EXPERTS, :]).then_inc(rows_kept, 16)
            sp.wait_ge(rows_kept, 16 * (i + 1))
            sp.dma_start(cwb[:, k], io["scratch_w"].rearrange("(a e) n -> a e n", a=1).broadcast_to([INTER, EXPERTS, TILE])).then_inc(rows_loaded, 16)

        def pe_hidden(pe, i, k, e):
            n = i * E1 + e
            if e >= 2:
                pe.wait_ge(g_ready, n - 1)
                pe.wait_ge(u_ready, n - 1)
            for half in range(2):
                nc.tensor.matmul(ps[0:INTER, 2 * half + e % 2, 0:TILE], w1[:, e, half, :], xn[:, k, :], start=True, stop=True).then_inc(h_sums, 1)

        def pe_out(pe, i, e):
            if e < EXPERTS:
                pe.wait_ge(weighted_ready, i * EXPERTS + e + 1)
                src = t3
            else:
                pe.wait_ge(product_ready, i * E1 + e + 1)
                src = t2
            last = nc.tensor.matmul(ps[:, 4, 0:TILE], w2[:, e, :], src[:, e % 2, :], start=False, stop=e == E1 - 1)
            last.then_inc(used, 1)

        def pe_step(pe, i, k, m, front):
            started(pe, i)
            nc.tensor.matmul(ps[:, 4, 0:TILE], b2[:], cwT[:], start=True, stop=False)
            pe_hidden(pe, i, k, 0)
            for e in range(1, E1):
                pe_hidden(pe, i, k, e)
                pe_out(pe, i, e - 1)
                if front and e == 1:
                    n0.pe_mean(hB[:, tile(i + 1)])
                if front and e == 4:
                    n0.pe_var(pe, i + 2)
                if front and e == 7:
                    pe_gate(pe, i + 1, 1 - k)
                if front and e == 13:
                    pe_rows(pe, i + 1)
            pe_out(pe, i, E1 - 1)

        def act_step(act, i, k, m, front):
            started(act, i)
            for e in range(E1):
                n = i * E1 + e
                act.wait_ge(g_ready, n + 1)
                if e >= 2:
                    act.wait_ge(gated_ready, n - 1)
                nc.scalar.activation(sg[:, e % 2, :], g0[:, e % 2, :], ACT.Sigmoid, bias=abias[:, e:e + 1], scale=acts[:, 0, e:e + 1]).then_inc(s_ready, 1)
                if front and e == 2:
                    n0.act_square(act, i + 2)
                if front and e == 4:
                    load_tables(nc, act, LN_EXP_SET)
                    n0.act_rstd(act, i + 2)
                    load_tables(nc, act, SIGMOID_SET)
                if front and e == 10:
                    act_route(act, i + 1)

        def dve_step(dve, i, k, m, front):
            v = nc.vector
            started(dve, i)
            for e in range(E1):
                n = i * E1 + e
                p = e % 2
                dve.wait_ge(h_sums, 2 * n + 1)
                if e >= 2:
                    dve.wait_ge(gated_ready, n - 1)
                v.tensor_scalar(g0[:, p, :], ps[0:INTER, p, 0:TILE], hi[:, 0, e:e + 1], lo[:, 0, e:e + 1], ALU.min, ALU.max).then_inc(g_ready, 1)
                dve.wait_ge(h_sums, 2 * n + 2)
                if e >= 2:
                    dve.wait_ge(product_ready, n - 1)
                v.tensor_scalar(u0[:, p, :], ps[0:INTER, 2 + p, 0:TILE], hi[:, 1, e:e + 1], lo[:, 1, e:e + 1], ALU.min, ALU.max).then_inc(u_ready, 1)
                dve.wait_ge(s_ready, n + 1)
                v.scalar_tensor_tensor(tt[:, p, :], g0[:, p, :], b1[:, 0, e:e + 1], sg[:, p, :], ALU.add, ALU.mult).then_inc(gated_ready, 1)
                dve.wait_ge(gated_ready, n + 1)
                dve.wait_ge(u_ready, n + 1)
                if e >= 2:
                    dve.wait_ge(weighted_ready, i * EXPERTS + e - 1)
                v.scalar_tensor_tensor(t2[:, p, :], u0[:, p, :], ushift[:, e:e + 1], tt[:, p, :], ALU.add, ALU.mult).then_inc(product_ready, 1)
                if front and e == 1:
                    n0.dve_center(dve, i + 2, hB[:, tile(i + 1)])
                if front and e == 6:
                    n0.dve_scale(dve, i + 2, xn[:, 1 - k, :])
                if front and e == 8:
                    dve_choose(dve, i + 1)
                if front and e == 12:
                    dve_weigh(dve, i + 1)
                if front and e == 15:
                    dve_rows(dve, i + 1)
            dve.wait_ge(used, E1 * (i + 1))
            dve.wait_ge(out_stored[k], 16 * m + 16)
            v.scalar_tensor_tensor(y[:, k, :], ps[:, 4, 0:TILE], b2s[:], hB[:, tile(i)], ALU.add, ALU.add).then_inc(y_ready, 1)

        def in_pairs(eng, step):
            with eng.Fori(0, TILES // 2 - 1) as m:
                for k in range(2):
                    step(eng, 2 * m + k, k, m, True)
            step(eng, TILES - 2, 0, TILES // 2 - 1, True)
            step(eng, TILES - 1, 1, TILES // 2 - 1, False)

        out_stored = [sem(f"e_out_stored{k}") for k in range(2)]
        with nc.Block() as block:
            @block.sync
            def _(sp):
                def step(sp, i, k, m, front):
                    if front:
                        sp_rows(sp, i + 1, 1 - k)
                    sp.wait_ge(y_ready, i + 2)
                    sp.dma_start(out[:, tile(i)], y[:, k, :]).then_inc(out_stored[k], 16)
                sp_rows(sp, 0, 0)
                in_pairs(sp, step)
                for k in range(2):
                    sp.wait_ge(out_stored[k], 16 * (TILES // 2 + 1))

            @block.tensor
            def _(pe):
                n0.pe_mean(hB[:, tile(0)])
                n0.pe_var(pe, 1)
                pe_gate(pe, 0, 0)
                pe_rows(pe, 0)
                in_pairs(pe, pe_step)

            @block.scalar
            def _(act):
                n0.act_square(act, 1)
                load_tables(nc, act, LN_EXP_SET)
                n0.act_rstd(act, 1)
                load_tables(nc, act, SIGMOID_SET)
                act_route(act, 0)
                in_pairs(act, act_step)

            @block.gpsimd
            def _(pool):
                def step(pool, i, k, m, front):
                    started(pool, i)
                    for e in range(EXPERTS):
                        n = i * E1 + e
                        if e >= 2:
                            pool.wait_ge(used, n - 1)
                        pool.wait_ge(product_ready, n + 1)
                        nc.gpsimd.tensor_tensor(t3[:, e % 2, :], t2[:, e % 2, :], cwb[:, k, e, :], ALU.mult).then_inc(weighted_ready, 1)
                        pool.wait_ge(weighted_ready, i * EXPERTS + e + 1)
                in_pairs(pool, step)

            @block.vector
            def _(dve):
                dve.sem_inc(y_ready, 1)
                for k in range(2):
                    dve.sem_inc(out_stored[k], 16)
                n0.dve_center(dve, 1, hB[:, tile(0)])
                n0.dve_scale(dve, 1, xn[:, 0, :])
                dve_choose(dve, 0)
                dve_weigh(dve, 0)
                dve_rows(dve, 0)
                in_pairs(dve, dve_step)


def build(nc, io, out, stages):
    with ExitStack() as top:
        sbt = lambda name, shape, dt=F32: top.enter_context(nc.sbuf_tensor(name, shape, dt))
        ps = top.enter_context(nc.psum_tensor("psum", [P, 8, BANK], F32))
        consts = sbt("consts", [P, 3 * P + 1 + GROUPS * P + 1])
        C = {"ones": consts[:, 0:P], "ident": consts[:, P:2 * P], "sel": consts[:, 2 * P:3 * P],
             "minus_row": consts[:, 3 * P:3 * P + 1], "ones_col": consts[:, 3 * P + 1:5 * P + 1], "eps": consts[:, 5 * P + 1:5 * P + 2]}
        C["loads"] = [(consts[:], io["consts"])]
        ident_bf = sbt("identity_bf16", [P, P], BF16)
        C["ident_bf"] = ident_bf
        hB = sbt("h_batch_major", [P, TOKENS])
        with ExitStack() as early:
            hA = early.enter_context(nc.sbuf_tensor("h_time_major", [P, TOKENS], F32))
            hn = early.enter_context(nc.sbuf_tensor("h_normed_parts", [P, 2, TOKENS], F16))
            stage_tokenizer(nc, io, hA, hB, ps, C)
            if stages >= 1:
                stage_cross_attention(nc, io, hA, hn, ps, C)
            if stages >= 2:
                stage_gru(nc, io, hA, hn, hB, ps, C)
            if stages <= 1:
                stored = early.enter_context(nc.semaphore("stored"))
                with nc.Block() as block:
                    @block.sync
                    def _(sp):
                        sp.dma_start(out, hA[:, :]).then_inc(stored, 16)
                        sp.wait_ge(stored, 16)
        if stages >= 3:
            stage_self_attention(nc, io, hB, ps, C)
        if stages >= 4:
            stage_experts(nc, io, out, hB, ps, C)
            return
        stored = top.enter_context(nc.semaphore("stored2"))
        with nc.Block() as block:
            @block.sync
            def _(sp):
                if stages in (2, 3):
                    sp.dma_start(out, hB[:, :]).then_inc(stored, 16)
                    sp.wait_ge(stored, 16)


def _pad(a, axis):
    a = np.moveaxis(a, axis, -1)
    o = np.zeros(a.shape[:-1] + (HEADS, SLOT), a.dtype)
    o[..., 0:HD] = a.reshape(a.shape[:-1] + (HEADS, HD))
    return np.moveaxis(o.reshape(a.shape[:-1] + (HEADS * SLOT,)), -1, axis)


def _constants():
    c = np.zeros((P, 5 * P + 2), np.float32)
    c[:, 0:P] = 1.0 / P
    c[:, P:2 * P] = np.eye(P)
    for j in range(GH):
        c[SLOT * j + HD, 2 * P + SLOT * j:2 * P + SLOT * (j + 1)] = 1.0
    c[HD::SLOT, 3 * P] = -1.0
    c[:, 3 * P + 1 + HD:5 * P + 1:SLOT] = 1.0
    c[:, 5 * P + 1] = LN_EPS
    return c


def _layout(a):
    t = np.transpose
    col = lambda v: v.reshape(-1, P).T
    io = {
        "consts": _constants(),
        "x": t(a["x"][:, 0:(STEPS + 1) * STRIDE].reshape(BATCH, STEPS + 1, STRIDE), (2, 1, 0)),
        "tok_W": a["L0_tok_W"], "tok_b": a["L0_tok_b"].reshape(P, 1), "tok_scale": a["L0_tok_effective_scale"].reshape(1, 1),
        "x_srcT": t(a["L0_attn_source_embedding"].reshape(SRC, KC, P), (2, 1, 0)),
        "x_valT": t(a["L0_attn_value_embedding"].reshape(SRC, KC, P), (2, 1, 0)),
        "x_WkT": t(a["L0_attn_Wk"].reshape(KC, P, P), (1, 0, 2)),
        "x_WvT": t(_pad(a["L0_attn_Wv"], 1).reshape(KC, P, GROUPS * P), (1, 0, 2)),
        "x_Wq": a["L0_attn_Wq"], "x_Wo": t(_pad(a["L0_attn_Wo"], 0).reshape(GROUPS, P, P), (1, 0, 2)),
        "x_bq": col(a["L0_attn_bq"]), "x_bk": col(a["L0_attn_bk"]), "x_bo": a["L0_attn_bo"].reshape(P, 1),
        "x_bv": _pad(a["L0_attn_bv"], 0).reshape(1, GROUPS * P),
    }
    gates = ("r", "z", "")
    sel = np.zeros((P, 2, BATCH), np.float32)
    for p in range(3):
        for m in range(2):
            sel[SLOT * p + m, m] = 1.0
    io.update({
        "g_Wx": np.concatenate([a["L0_ffn_Wu" + g].T for g in gates], 1),
        "g_Wh": t(np.stack([a["L0_ffn_Ww" + g].T.reshape(2, P, HID) for g in gates]), (2, 1, 0, 3)).reshape(P, -1),
        "g_Wo": t(a["L0_ffn_Wo"].T.reshape(2, P, P), (1, 0, 2)).reshape(P, -1), "g_bo": a["L0_ffn_bo"].reshape(P, 1),
        "g_sel": sel.reshape(P, 2 * BATCH),
        "g_b": t(np.stack([np.stack([a[n + g].reshape(2, P) for g in gates]) for n in ("L0_ffn_bu", "L0_ffn_bw")]), (2, 0, 1, 3)),
    })
    turn = (np.arange(D) // HD) * HD + (np.arange(D) + HD // 2) % HD
    wq, wk, KN = a["L1_attn_Wq"].T, a["L1_attn_Wk"].T, (STEPS + 1) // 2
    freq = np.float32(1.0) / np.float32(10000.0) ** (np.arange(0, HD, 2, dtype=np.float32) / np.float32(HD))
    angle = np.arange(STEPS, dtype=np.float32)[None, :] * freq[:, None]
    cos, sin = np.cos(angle), np.sin(angle)
    rope = np.stack([np.tile(np.concatenate([cos, cos]), (HEADS, 2)), np.tile(np.concatenate([-sin, sin]), (HEADS, 2))], 1)
    vmask = np.ones((KN, 2), np.float32)
    vmask[0, 1] = 0.0
    vpat = np.zeros((KN, 2, 2 * HEADS, SLOT), np.float32)
    vpat[:, :, :, HD] = vmask[:, :, None]
    io.update({
        "s_wqk": np.stack([wq, wq[:, turn], wk, wk[:, turn]], 1),
        "s_wv": _pad(a["L1_attn_Wv"].T, 1), "s_wo": t(_pad(a["L1_attn_Wo"].T, 0).reshape(GROUPS, P, P), (1, 0, 2)),
        "s_w1": a["L1_attn_W1"].T.reshape(P, DFF // P, P), "s_w2": t(a["L1_attn_W2"].T.reshape(DFF // P, P, P), (1, 0, 2)),
        "s_columns": np.concatenate([col(a["L1_attn_b1"])] + [a["L1_attn_" + n].reshape(P, 1) for n in ("b2", "g1", "be1", "g2", "be2")], 1),
        "s_rope": rope, "s_vmask": vmask, "s_vpat": vpat.reshape(KN, 2, -1),
    })
    w1 = np.concatenate([a["L1_ffn_expert_w1"], a["L1_ffn_shared_w1"][None]])
    b1 = np.concatenate([a["L1_ffn_expert_b1"], a["L1_ffn_shared_b1"][None]])
    w2 = np.concatenate([a["L1_ffn_expert_w2"], a["L1_ffn_shared_w2"][None]])
    act = np.concatenate([a["L1_ffn_expert_act"], a["L1_ffn_shared_act"][None]])
    b2 = np.zeros((P, P), np.float32)
    b2[0:EXPERTS] = a["L1_ffn_expert_b2"]
    io.update({
        "e_w1": t(w1.reshape(EXPERTS + 1, P, INTER, 2), (1, 0, 3, 2)), "e_w2": t(w2, (1, 0, 2)), "e_b1": t(b1.reshape(EXPERTS + 1, INTER, 2), (1, 2, 0)),
        "e_gate_w": a["L1_ffn_gate_w"], "e_gate_b": a["L1_ffn_gate_b"].reshape(1, 1, EXPERTS),
        "e_rank": np.arange(EXPERTS, 0, -1, dtype=np.float32).reshape(1, 1, EXPERTS),
        "e_act": act.T.reshape(1, 5, EXPERTS + 1), "e_b2": b2, "e_b2s": a["L1_ffn_shared_b2"].reshape(P, 1),
    })
    return io


STAGES = 4


def kernel(**inputs):
    import concourse.bacc as bacc
    from concourse.bass_utils import run_bass_kernel_spmd

    nc = bacc.Bacc("TRN2", target_bir_lowering=False, num_devices=1)
    arrays, io = {}, {}
    for name, a in _layout({k: np.asarray(v) for k, v in inputs.items()}).items():
        a = np.ascontiguousarray(a)
        arrays["in_" + name] = a
        io[name] = nc.dram_tensor("in_" + name, a.shape, mybir.dt.from_np(a.dtype), kind="ExternalInput").ap()
    for name, width in (("scratch_q", 3 * TILE), ("scratch_k", 3 * TILE)):
        io[name] = nc.dram_tensor(name, (P, width), BF16).ap().rearrange("p (a n) -> p a n", a=3)
    io["scratch_m"] = nc.dram_tensor("scratch_m", (3 * HEADS, TILE), BF16).ap()
    io["scratch_w"] = nc.dram_tensor("scratch_w", (EXPERTS, TILE), F32).ap()
    out = nc.dram_tensor("out_features", (P, TOKENS), F32, kind="ExternalOutput").ap()
    build(nc, io, out, STAGES)
    r = run_bass_kernel_spmd(nc, [arrays], core_ids=[0])
    y = r.results[0]["out_features"]
    if STAGES <= 1:
        return np.ascontiguousarray(y.reshape(P, STEPS, BATCH).transpose(2, 1, 0))
    return np.ascontiguousarray(y.reshape(P, BATCH, STEPS).transpose(1, 2, 0))
```
